# Optimizing a Trainium2 kernel written in Bass

```python
import numpy as np
import jax
import jax.numpy as jnp

def _softmax(x, axis=-1):
    return jax.nn.softmax(x, axis=axis)

def _gelu(x):
    return jax.nn.gelu(x, approximate=True)

def _silu(x):
    return jax.nn.silu(x)

def _sigmoid(x):
    return jax.nn.sigmoid(x)

def _layernorm(x, axis=-1, eps=1e-05):
    m = jnp.mean(x, axis=axis, keepdims=True)
    v = jnp.var(x, axis=axis, keepdims=True)
    return (x - m) / jnp.sqrt(v + eps)

def _scatter_add(tgt, idx, src, axis=0):
    return tgt.at[idx].add(src)

def _segment_sum(src, seg, n):
    return jax.ops.segment_sum(src, seg, n)
kernel_name = 'mk_adj_resnorm_d4_adj_r2_8c1f83'

def setup_inputs(seed: int=0):
    np.random.seed(seed)
    _w = jnp.asarray

    def _rec_inputs():
        import jax
        import jax.numpy as jnp
        _gk = jax.random.key(seed)
        x = 7.22e-05 + 1 * jax.random.normal(jax.random.fold_in(_gk, 1), (8, 1024, 128), jnp.float32)
        _a = jax.random.bernoulli(jax.random.fold_in(_gk, 2), 0.00390625, (8, 1024, 1024))
        _a = jnp.logical_or(_a, jnp.swapaxes(_a, -1, -2))
        _a = jnp.logical_or(_a, jnp.eye(1024, dtype=bool))
        _af = _a.astype(jnp.float32)
        adj = _af
        return (x, adj)
    x, adj = _rec_inputs()

    def _L0_gnn_setup():
        import jax, jax.numpy as jnp
        import numpy as np
        B, S, HID = (64, 512, 128)
        NH, DH = (1, 128)
        SCALE = 1.0 / float(np.sqrt(DH))
        NEG = -10000.0
        key = jax.random.key(seed)
        k1, k2, k3, k4, k5, k6 = jax.random.split(key, 6)
        return {'hidden_states': jax.random.normal(k1, (B, S, HID), dtype=jnp.float32), 'attention_mask': jnp.ones((B, S, S), dtype=jnp.float32), 'Wq': jax.random.normal(k2, (HID, HID), dtype=jnp.float32) * 0.05, 'bq': jax.random.normal(k3, (HID,), dtype=jnp.float32) * 0.05, 'Wk': jax.random.normal(k4, (HID, HID), dtype=jnp.float32) * 0.05, 'Wv': jax.random.normal(k5, (HID, HID), dtype=jnp.float32) * 0.05, 'bv': jax.random.normal(k6, (HID,), dtype=jnp.float32) * 0.05}
    _L0_gnn_all = _L0_gnn_setup()
    _L0_gnn_in = {k: v for k, v in _L0_gnn_all.items() if k in ('Wq', 'bq', 'Wk', 'Wv', 'bv')}
    del _L0_gnn_all

    def _L1_gnn_setup():
        import jax, jax.numpy as jnp
        import numpy as np
        B, N, FIN, FOUT = (32, 512, 128, 128)
        NEG_SLOPE = 0.01
        key = jax.random.key(seed)
        k1, k2, k3, k4 = jax.random.split(key, 4)
        node_mat = jax.random.normal(k1, (B, N, FIN), dtype=jnp.float32)
        adj_mat = jax.random.uniform(k2, (B, N, N), dtype=jnp.float32)
        bound = 1.0 / np.sqrt(FIN)
        W = jax.random.uniform(k3, (FOUT, FIN), minval=-bound, maxval=bound, dtype=jnp.float32)
        b = jax.random.uniform(k4, (FOUT,), minval=-bound, maxval=bound, dtype=jnp.float32)
        return {'node_mat': node_mat, 'adj_mat': adj_mat, 'W': W, 'b': b}
    _L1_gnn_all = _L1_gnn_setup()
    _L1_gnn_in = {k: v for k, v in _L1_gnn_all.items() if k in ('W', 'b')}
    del _L1_gnn_all

    def _L2_gnn_setup():
        import jax, jax.numpy as jnp
        import numpy as np
        NEG_SLOPE = 0.2
        MASK_EPS = 1e-08
        NEG_INF = -1000000000.0
        key = jax.random.key(seed)
        k1, k2, k3, k4 = jax.random.split(key, 4)
        B, N, D_in, D_out, H = (32, 256, 128, 128, 4)
        h = jax.random.normal(k1, (B, N, D_in), dtype=jnp.float32)
        adj = jax.random.uniform(k2, (B, N, N), dtype=jnp.float32)
        W = jax.random.normal(k3, (D_in, D_out), dtype=jnp.float32) * (1.0 / np.sqrt(D_in))
        a = jax.random.normal(k4, (H, 2 * (D_out // H)), dtype=jnp.float32) * 0.1
        return {'h': h, 'adj': adj, 'W': W, 'a': a}
    _L2_gnn_all = _L2_gnn_setup()
    _L2_gnn_in = {k: v for k, v in _L2_gnn_all.items() if k in ('W', 'a')}
    del _L2_gnn_all

    def _L3_gnn_setup():
        import jax, jax.numpy as jnp
        import numpy as np
        key = jax.random.key(seed)
        k1, k2, k3 = jax.random.split(key, 3)
        B_, N, F, O = (8, 1024, 128, 128)
        H = jax.random.normal(k1, (B_, N, F), dtype=jnp.float32)
        A = jax.random.uniform(k2, (B_, N, N), dtype=jnp.float32)
        B = jax.random.normal(k3, (F, O), dtype=jnp.float32) / np.sqrt(F)
        return {'H': H, 'A': A, 'B': B}
    _L3_gnn_all = _L3_gnn_setup()
    _L3_gnn_in = {k: v for k, v in _L3_gnn_all.items() if k in ('B',)}
    del _L3_gnn_all
    return {'x': x, 'adj': adj, 'L0_gnn_Wq': _L0_gnn_in['Wq'], 'L0_gnn_bq': _L0_gnn_in['bq'], 'L0_gnn_Wk': _L0_gnn_in['Wk'], 'L0_gnn_Wv': _L0_gnn_in['Wv'], 'L0_gnn_bv': _L0_gnn_in['bv'], 'L1_gnn_W': _L1_gnn_in['W'], 'L1_gnn_b': _L1_gnn_in['b'], 'L2_gnn_W': _L2_gnn_in['W'], 'L2_gnn_a': _L2_gnn_in['a'], 'L3_gnn_B': _L3_gnn_in['B']}

def reference(x, adj, L0_gnn_Wq, L0_gnn_bq, L0_gnn_Wk, L0_gnn_Wv, L0_gnn_bv, L1_gnn_W, L1_gnn_b, L2_gnn_W, L2_gnn_a, L3_gnn_B):
    import jax
    import jax.numpy as jnp

    def _L0_gnn_ref(hidden_states, attention_mask, Wq, bq, Wk, Wv, bv):
        import jax, jax.numpy as jnp
        import numpy as np
        B, S, HID = (64, 512, 128)
        NH, DH = (1, 128)
        SCALE = 1.0 / float(np.sqrt(DH))
        NEG = -10000.0
        b, s, _ = hidden_states.shape
        q = hidden_states @ Wq.T + bq
        k = hidden_states @ Wk.T
        v = hidden_states @ Wv.T + bv
        q = q.reshape(b, s, NH, DH).transpose(0, 2, 1, 3)
        k = k.reshape(b, s, NH, DH).transpose(0, 2, 1, 3)
        v = v.reshape(b, s, NH, DH).transpose(0, 2, 1, 3)
        scores = jnp.einsum('bhqd,bhkd->bhqk', q * SCALE, k)
        scores = scores + (1.0 - attention_mask)[:, None, :, :] * NEG
        probs = jax.nn.softmax(scores, axis=-1)
        ctx = jnp.einsum('bhqk,bhkd->bhqd', probs, v)
        return ctx.transpose(0, 2, 1, 3).reshape(b, s, NH * DH)

    def _L1_gnn_ref(node_mat, adj_mat, W, b):
        import jax, jax.numpy as jnp
        import numpy as np
        B, N, FIN, FOUT = (32, 512, 128, 128)
        NEG_SLOPE = 0.01
        n_neighbors = adj_mat.sum(axis=-1, keepdims=True)
        norm_adj = adj_mat / n_neighbors
        agg = jnp.einsum('bnm,bmf->bnf', norm_adj, node_mat)
        out = jnp.einsum('bnf,of->bno', agg, W) + b
        return jnp.where(out >= 0, out, NEG_SLOPE * out)

    def _L2_gnn_ref(h, adj, W, a):
        import jax, jax.numpy as jnp
        import numpy as np
        NEG_SLOPE = 0.2
        MASK_EPS = 1e-08
        NEG_INF = -1000000000.0
        B, N, _ = h.shape
        H, two_dh = a.shape
        Dh = two_dh // 2
        Wh = (h @ W).reshape(B, N, H, Dh)
        a_src, a_dst = (a[:, :Dh], a[:, Dh:])
        s_i = jnp.einsum('bnhd,hd->bnh', Wh, a_src)
        s_j = jnp.einsum('bnhd,hd->bnh', Wh, a_dst)
        e = s_i[:, :, None, :] + s_j[:, None, :, :]
        e = jnp.where(e >= 0, e, NEG_SLOPE * e)
        mask = adj[..., None] > MASK_EPS
        e = jnp.where(mask, e, NEG_INF)
        alpha = jax.nn.softmax(e, axis=-3)
        out = jnp.einsum('bijh,bihd->bjhd', alpha, Wh)
        return out.reshape(B, N, H * Dh)

    def _L3_gnn_ref(H, A, B):
        import jax, jax.numpy as jnp
        import numpy as np
        N = A.shape[-1]
        A1 = A + jnp.eye(N, dtype=A.dtype)
        deg = jnp.sum(A1, axis=-1)
        d = jax.lax.rsqrt(deg)
        A_norm = A1 * d[:, :, None] * d[:, None, :]
        HB = jnp.matmul(A_norm, H)
        return jnp.matmul(HB, B)
    x = _layernorm(x + _L0_gnn_ref(x, adj, L0_gnn_Wq, L0_gnn_bq, L0_gnn_Wk, L0_gnn_Wv, L0_gnn_bv), axis=-1)
    x = _layernorm(x + _L1_gnn_ref(x, adj, L1_gnn_W, L1_gnn_b), axis=-1)
    x = _layernorm(x + _L2_gnn_ref(x, adj, L2_gnn_W, L2_gnn_a), axis=-1)
    x = _layernorm(x + _L3_gnn_ref(x, adj, L3_gnn_B), axis=-1)
    return x

_drawn_inputs = setup_inputs


def setup_inputs(seed=0):
    import zlib

    import numpy as np

    out = dict(_drawn_inputs(seed))
    spreads = {}
    factors = {'L0_gnn_bq': 8.0}
    for name, (base, spread) in spreads.items():
        noise = np.random.default_rng([zlib.crc32(name.encode()), seed]).standard_normal(out[name].shape)
        drawn = base * np.exp(spread * noise) if base else spread * noise
        out[name] = jnp.asarray(drawn.astype(out[name].dtype))
    for name, factor in factors.items():
        out[name] = (out[name] * factor).astype(out[name].dtype)
    return out
```

```python
from contextlib import ExitStack

import concourse.bass as bass
from concourse import mybir

F32 = mybir.dt.float32
F16 = mybir.dt.float16
BF16 = mybir.dt.bfloat16
ALU = mybir.AluOpType
ACT = mybir.ActivationFunctionType
AX_X = mybir.AxisListType.X
RMAX = bass.bass_isa.ReduceOp.max

P = 128
EPS = 1e-5
NEG = 10000.0
STEEP = 1e20
SLOPE1 = 0.01
SLOPE2 = 0.2
LOWEST = -3.0e38


class Graph:

    def __init__(self, base, turn=None):
        self.base, self.turn = base, turn
        self.parity = base % 2

    def before(self, n=1):
        return Graph(self.base - n, self.turn)

    def count(self, per, k=0):
        n = self.base * per + k
        return n if self.turn is None else self.turn * (2 * per) + n

    def count_own(self, per, k):
        n = (self.base // 2) * per + k
        return n if self.turn is None else self.turn * per + n


def gnn_kernel(nc, x, adj, WqT, bq, WkT, WvT, bv, W1T, b1, W2, a2, B3, out):
    NB, N, D = x.shape
    T = N // P
    H = a2.shape[0]
    DH = D // H
    SCALE = float(D) ** -0.5
    VW = 2 * DH + 2
    HW = DH + 1
    assert D == P and T == 8 and NB % 2 == 0

    x_v = x.rearrange("b (t p) d -> b p t d", p=P)
    adj_v = adj.rearrange("b (t p) m -> b p t m", p=P)
    out_v = out.rearrange("b (t p) d -> b p t d", p=P)

    first_half = [("xT", 0), ("q", 0), ("k", 0), ("v", 0)] + [("at", m) for m in range(T)]
    score = [("s", t) for t in range(T)]
    heads_up = [("x2T", 0), ("wh", 0), ("wh", 1), ("bc", 0), ("bc", 1)]
    mixed = [g for pair in zip(score, heads_up) for g in pair] + score[len(heads_up):]
    soft = [("st", g) for g in range(T)]
    gat = [("bc", 2), ("bc", 3), ("mask", 0), ("mask", 1)] + [("c", g) for g in range(2 * H)]
    ORDER = {
        "first": first_half + score + soft + [("out1", 0), ("out1", 1)],
        "full": first_half + mixed + soft + gat + [("out1", 0), ("out1", 1), ("out3", 0)],
        "last": heads_up + gat + [("out3", 0)],
    }
    SLOTS = 3
    assert len(ORDER["first"]) % SLOTS == 0 and len(ORDER["full"]) % SLOTS == 0
    OLDER = ("x2T", "wh", "bc", "mask", "c", "out3")

    ctx = ExitStack()
    with ctx:
        def sb(name, shape, dt):
            return ctx.enter_context(nc.sbuf_tensor(name, shape, dt))

        def sem(name):
            return ctx.enter_context(nc.semaphore(name))

        adjs = [sb(f"adj{p}", [P, T, N], F16) for p in range(2)]
        adjTs = [sb(f"adjT{p}", [P, T, N], F16) for p in range(2)]
        maskb = sb("maskb", [P, T, N], F16)
        cmat = sb("cmat", [P, 2, T, N], BF16)
        vals = cmat[:, 1, :, :].rearrange("p t n -> p (t n)")[:, 0:2 * T * H * VW].bitcast(F32)\
            .rearrange("p (t h c) -> p t h c", h=H, c=VW)
        probs = sb("probs", [P, 2, 2, 512], F32)
        msum = probs[:, :, :, :].rearrange("p a b c -> p (a b c)")[:, 0:T * H * HW]\
            .rearrange("p (t c) -> p t c", t=T)
        x0 = sb("x0", [P, T, D], F32)
        x1 = sb("x1", [P, T, D], F32)
        x2 = sb("x2", [P, T, D], F32)
        x3 = sb("x3", [P, T, D], F32)
        parts1 = sb("parts1", [P, 3, T, D], BF16)
        xT = sb("xT", [P, N], F32)
        qT = sb("qT", [P, N], F32)
        kT = sb("kT", [P, N], F32)
        agg1T, agg3T = qT, kT
        vparts = sb("vparts", [P, T, H, 3, VW], BF16)
        flat = vparts[:, :, :, :, :].rearrange("p t h s c -> p (t h s c)")
        qb, kb = flat[:, 0:N], flat[:, N:2 * N]
        parts3 = flat[:, 0:3 * N].rearrange("p (s t d) -> p s t d", s=3, d=D)
        vv = sb("vv", [P, T, D + 1], F32)
        negmax = sb("negmax", [P, N], BF16)
        wh = sb("wh", [P, T, D + 2 * H], F32)
        sjrow = sb("sjrow", [P, 2, N], F32)
        steps = sb("steps", [P, 2, N], BF16)
        csum = sb("csum", [P, 2, T, VW], F32)
        abc = csum[:, 0, :, :].rearrange("p t c -> p (t c)")[:, 0:2 * D]\
            .rearrange("p (h s d) -> p h s d", h=H, s=2)
        num = sb("num", [P, T, HW], F32)
        num2 = sb("num2", [P, T, HW], F32)
        gatout = sb("gatout", [P, T, DH], F32)
        rest = sb("rest", [P, 4 * D], F32)

        identf = sb("identf", [P, P], F32)
        ident16 = sb("ident16", [P, P], F16)
        identb = sb("identb", [P, P], BF16)
        onesb = sb("onesb", [P, P], BF16)
        wq_s = sb("wq_s", [P, D], F32)
        wk_s = sb("wk_s", [P, D], F32)
        wv_s = sb("wv_s", [P, D], F32)
        w1_s = sb("w1_s", [P, D], F32)
        b3_s = sb("b3_s", [P, D], F32)
        wext = sb("wext", [P, D + 2 * H], F32)
        wdst = sb("wdst", [P, H, P], F32)
        bv_s = sb("bv_s", [P, D], F32)
        b1_s = sb("b1_s", [P, D], F32)
        bqcol = sb("bqcol", [P, 2], F32)
        negcol = sb("negcol", [P, 1], F32)
        powers = sb("powers", [P, T, 2], F32)

        rowacc = sb("rowacc", [P, T], F32)
        rowsum = sb("rowsum", [P, T], F32)
        degree = sb("degree", [P, T], F32)
        rrow = sb("rrow", [P, T], F32)
        dcol = [sb(f"dcol{p}", [P, T], F32) for p in range(2)]
        smax = sb("smax", [P, T], F32)
        rden = sb("rden", [P, T], F32)
        rgat = sb("rgat", [P, T], F32)
        mloc = sb("mloc", [P, H], F32)
        mall = sb("mall", [P, H], F32)
        wsj = sb("wsj", [P, T, H], F32)
        exin = sb("exin", [P, 4, T, H], F32)
        ex = sb("ex", [P, 4, T, H], F32)
        steepsi = sb("steepsi", [P, T, H], F32)
        stats = sb("stats", [P, T, 6], F32)
        meanvar = sb("meanvar", [P, 4, T, 2], F32)
        vareps = sb("vareps", [P, 4, T], F32)
        rstd = sb("rstd", [P, 4, T], F32)

        ring = [ctx.enter_context(nc.psum_tensor(f"ring{s}", [P, 2, 512], F32)) for s in range(SLOTS)]
        Z = ctx.enter_context(nc.psum_tensor("Z", [P, 2, 512], F32))

        consts_in = sem("consts_in")
        x_in = sem("x_in")
        adj_in = [sem("adj_in0"), sem("adj_in1")]
        stored = sem("stored")
        ident_made = sem("ident_made")
        dve_init = sem("dve_init")
        pool_init = sem("pool_init")
        act_init = sem("act_init")
        full = {n: sem(f"{n}_full") for n in
                ("xT", "q", "k", "v", "at", "s", "st", "agg1", "out1", "x2T", "wh", "bc", "mask", "c", "agg3", "out3")}
        read = {n: sem(f"{n}_read") for n in full if n != "out3"}
        PER = {"xT": 1, "q": 1, "k": 1, "v": 1, "at": T, "s": T, "st": T, "agg1": 1, "out1": 2,
               "x2T": 1, "wh": 2, "bc": H, "mask": 2, "c": 2 * H, "agg3": 1}
        x0_biased = sem("x0_biased")
        maskb_made = sem("maskb_made")
        degrees = sem("degrees")
        negmax_made = sem("negmax_made")
        probs_used = sem("probs_used")
        rden_made = sem("rden_made")
        y_made = [sem(f"y_made{n}") for n in range(4)]
        stats_made = [sem(f"stats_made{n}") for n in range(4)]
        meanvar_made = [sem(f"meanvar_made{n}") for n in range(4)]
        vareps_made = [sem(f"vareps_made{n}") for n in range(4)]
        rstd_made = [sem(f"rstd_made{n}") for n in range(4)]
        normed = [sem(f"normed{n}") for n in range(4)]
        split1 = sem("split1")
        split3 = sem("split3")
        z1_made = sem("z1_made")
        mloc_made = sem("mloc_made")
        mall_made = sem("mall_made")
        exin_made = sem("exin_made")
        ex_made = sem("ex_made")
        vals_made = sem("vals_made")
        vsplit = sem("vsplit")
        step_made = sem("step_made")
        c_made = sem("c_made")
        num_made = sem("num_made")
        rgat_made = sem("rgat_made")
        gat_made = sem("gat_made")
        diag_added = sem("diag_added")

        CONSTS = 12
        block = ctx.enter_context(nc.Block())

        def slot(kind, name, k):
            return ring[ORDER[kind].index((name, k)) % SLOTS]

        def quarter(slot_, n):
            return slot_[:, n // 2, (n % 2) * 256:(n % 2) * 256 + 256]

        def quarters(slot_):
            return slot_[:, :, :].rearrange("p b (a c) -> p (b a) c", a=2)

        def whole(slot_):
            return slot_[:, :, :].rearrange("p b c -> p (b c)")

        def by_tile(slot_):
            return whole(slot_).rearrange("p (t c) -> p t c", c=P)

        def program(engine, step):
            step("first", Graph(0))
            step("full", Graph(1))
            with engine.Fori(0, NB // 2 - 2) as turn:
                step("full", Graph(2, turn))
                step("full", Graph(3, turn))
            step("full", Graph(NB - 2))
            step("full", Graph(NB - 1))
            step("last", Graph(NB))

        @block.sync
        def _(sp):
            for dst, src in ((wq_s, WqT), (wk_s, WkT), (wv_s, WvT), (w1_s, W1T), (b3_s, B3)):
                sp.dma_start(dst[:, :], src).then_inc(consts_in, 16)
            sp.dma_start(wext[:, 0:D], W2).then_inc(consts_in, 16)
            sp.dma_start(bqcol[:, 0:1], bq.rearrange("(p a) -> p a", a=1)).then_inc(consts_in, 16)
            for dst, src in ((bv_s, bv), (b1_s, b1)):
                sp.dma_start(dst[:, :], src.rearrange("(a d) -> a d", a=1).broadcast_to([P, D])).then_inc(consts_in, 16)
            sp.dma_start(csum[:, 0, :, :].rearrange("p t c -> p (t c)")[:, 0:2 * D],
                         a2.rearrange("(a h) c -> a (h c)", a=1).broadcast_to([P, 2 * D])).then_inc(consts_in, 16)
            sp.dma_start(x0[:, :, :], x_v[0]).then_inc(x_in, 16)

            def step(kind, g):
                if kind == "last":
                    sp.wait_ge(normed[3], g.before().count(2, 2))
                    sp.dma_start(out_v[NB - 1], x3[:, :, :]).then_inc(stored, 16)
                    return
                if g.turn is not None or g.base < NB - 1:
                    sp.wait_ge(y_made[0], g.count(2, 2))
                    n = g.base + 1 if g.turn is None else g.turn * 2 + (g.base + 1)
                    sp.dma_start(x0[:, :, :], x_v[n]).then_inc(x_in, 16)
                if kind == "full":
                    sp.wait_ge(normed[3], g.before().count(2, 2))
                    n = g.base - 1 if g.turn is None else g.turn * 2 + (g.base - 1)
                    sp.dma_start(out_v[n], x3[:, :, :]).then_inc(stored, 16)

            program(sp, step)
            sp.wait_ge(stored, 16 * NB)

        @block.gpsimd
        def _(pool):
            def load_adj(g):
                n = g.base if g.turn is None else g.turn * 2 + g.base
                pool.dma_start(adjs[g.parity][:, :, :], adj_v[n]).then_inc(adj_in[g.parity], 16)

            load_adj(Graph(0))
            pool.memset(identf[:, :], 0.0).then_inc(ident_made, 1)
            pool.wait_ge(ident_made, 1)
            pool.affine_select(out=identf[:, :], in_=identf[:, :], compare_op=ALU.not_equal, fill=1.0,
                               base=0, pattern=[[-1, P]], channel_multiplier=1).then_inc(ident_made, 1)
            load_adj(Graph(1))
            pool.memset(powers[:, :, 0], -0.5).then_inc(pool_init, 1)
            pool.memset(powers[:, :, 1], -1.0).then_inc(pool_init, 1)
            pool.memset(negcol[:, :], -NEG).then_inc(pool_init, 1)
            pool.memset(vv[:, :, D:D + 1], 1.0).then_inc(pool_init, 1)
            pool.memset(onesb[:, :], 1.0).then_inc(pool_init, 1)
            pool.wait_ge(pool_init, 5)
            pool.wait_ge(consts_in, 16 * 10)

            def bias_x0(g):
                pool.wait_ge(full["xT"], g.count(1, 1))
                pool.tensor_tensor(x0[:, :, :], x0[:, :, :], bv_s[:, :].unsqueeze(1).broadcast_to([P, T, D]),
                                   ALU.add).then_inc(x0_biased, 1)

            def degree_of(g):
                pool.wait_ge(maskb_made, g.count(T, T))
                pool.nop(nofuse=True)
                pool.tensor_scalar(rowsum[:, :], rowacc[:, :], N * NEG, 1.0 / NEG, ALU.add, ALU.mult).then_inc(degrees, 1)
                pool.wait_ge(degrees, g.count(4, 1))
                pool.nop(nofuse=True)
                pool.tensor_scalar(degree[:, :], rowsum[:, :], 1.0, None, ALU.add).then_inc(degrees, 1)
                pool.tensor_tensor(rrow[:, :], rowsum[:, :], powers[:, :, 1], ALU.pow).then_inc(degrees, 1)
                pool.wait_ge(degrees, g.count(4, 2))
                pool.tensor_tensor(dcol[g.parity][:, :], degree[:, :], powers[:, :, 0], ALU.pow).then_inc(degrees, 1)

            def rstd_of(layer, g):
                for k in range(2):
                    ts = slice(4 * k, 4 * k + 4)
                    pool.wait_ge(meanvar_made[layer], g.count(2, k + 1))
                    pool.nop(nofuse=True)
                    pool.tensor_scalar(vareps[:, layer, ts], meanvar[:, layer, ts, 1], EPS, None, ALU.add)\
                        .then_inc(vareps_made[layer], 1)
                    pool.wait_ge(vareps_made[layer], g.count(2, k + 1))
                    pool.tensor_tensor(rstd[:, layer, ts], vareps[:, layer, ts], powers[:, 0:4, 0], ALU.pow)\
                        .then_inc(rstd_made[layer], 1)

            def values_of(o):
                pool.wait_ge(mloc_made, o.count(1, 1))
                pool.nop(nofuse=True)
                pool.partition_all_reduce(mall[:, :], mloc[:, :], P, RMAX).then_inc(mall_made, 1)
                pool.wait_ge(ex_made, o.count(1, 1))
                heads = wh[:, :, 0:D].rearrange("p t (h d) -> p t h d", h=H)
                for n in range(2):
                    at = n * HW
                    pool.tensor_tensor(vals[:, :, :, at:at + DH], heads,
                                       ex[:, n, :, :].unsqueeze(3).broadcast_to([P, T, H, DH]), ALU.mult)\
                        .then_inc(vals_made, 1)
                    pool.tensor_copy(vals[:, :, :, at + DH], ex[:, n, :, :]).then_inc(vals_made, 1)

            def combine_heads(o):
                for h in range(H):
                    pool.wait_ge(read["c"], o.count(2 * H, 2 * h + 2))
                    if h == 0:
                        pool.wait_ge(read["mask"], o.count(2, 2))
                    else:
                        pool.wait_ge(rgat_made, o.count(H, h))
                        pool.wait_ge(gat_made, o.count(H, h))
                    cs = csum[:, h % 2, :, :]
                    f = [ex[:, 2 + n, :, h].unsqueeze(2).broadcast_to([P, T, HW]) for n in range(2)]
                    pool.tensor_tensor(num[:, :, :], msum[:, :, h * HW:(h + 1) * HW], cs[:, :, HW:VW], ALU.subtract)\
                        .then_inc(num_made, 1)
                    pool.tensor_tensor(num2[:, :, :], cs[:, :, 0:HW], f[0], ALU.mult).then_inc(num_made, 1)
                    pool.wait_ge(num_made, o.count(4 * H, 4 * h + 1))
                    pool.tensor_tensor(num[:, :, :], num[:, :, :], f[1], ALU.mult).then_inc(num_made, 1)
                    pool.wait_ge(num_made, o.count(4 * H, 4 * h + 3))
                    pool.tensor_tensor(num[:, :, :], num[:, :, :], num2[:, :, :], ALU.add).then_inc(num_made, 1)

            def add_diagonal(g):
                pool.wait_ge(full["agg1"], g.count(1, 1))
                for t in range(T):
                    d = adjTs[g.parity][:, t, t * P:(t + 1) * P]
                    ins = pool.tensor_tensor(d, d, ident16[:, :], ALU.add)
                ins.then_inc(diag_added, 1)

            def step(kind, g):
                o = g.before()
                if kind != "last":
                    bias_x0(g)
                    degree_of(g)
                if kind != "first":
                    values_of(o)
                if kind != "last":
                    rstd_of(0, g)
                if kind != "first":
                    combine_heads(o)
                    rstd_of(2, o)
                    if kind == "full" and (g.turn is not None or g.base < NB - 1):
                        pool.wait_ge(read["c"], o.count(2 * H, 2 * H))
                        load_adj(Graph(g.base + 1, g.turn))
                if kind != "last":
                    add_diagonal(g)
                    rstd_of(1, g)
                if kind != "first":
                    rstd_of(3, o)

            program(pool, step)

        @block.scalar
        def _(act):
            act.wait_ge(consts_in, 16 * 10)
            act.activation(bqcol[:, 1:2], bqcol[:, 0:1], ACT.Copy, scale=SCALE).then_inc(act_init, 1)
            act.wait_ge(act_init, 1)
            act.wait_ge(pool_init, 5)

            def make_maskb(g):
                act.wait_ge(adj_in[g.parity], g.count_own(16, 16))
                if g.turn is not None or g.base > 0:
                    act.wait_ge(full["st"], g.count(T))
                    act.wait_ge(degrees, g.count(4))
                for t in range(T):
                    act.activation(maskb[:, t, :], adjs[g.parity][:, t, :], ACT.Identity, bias=negcol[:, :], scale=NEG,
                                   accum_out=rowacc[:, t:t + 1]).then_inc(maskb_made, 1)

            def take(kind, g, name, k, dst, src):
                act.wait_ge(full[name], g.count(PER[name], k + 1))
                return act.activation(dst, src, ACT.Copy)

            def project(kind, g):
                take(kind, g, "xT", 0, xT[:, :], whole(slot(kind, "xT", 0))).then_inc(read["xT"], 1)
                src = whole(slot(kind, "q", 0))
                act.wait_ge(full["q"], g.count(1, 1))
                act.activation(qT[:, :], src, ACT.Identity, bias=bqcol[:, 1:2], scale=SCALE)
                act.activation(qb, src, ACT.Identity, bias=bqcol[:, 1:2], scale=SCALE).then_inc(read["q"], 1)
                src = whole(slot(kind, "k", 0))
                take(kind, g, "k", 0, kT[:, :], src)
                act.activation(kb, src, ACT.Copy).then_inc(read["k"], 1)
                take(kind, g, "v", 0, vv[:, :, 0:D], by_tile(slot(kind, "v", 0))).then_inc(read["v"], 1)
                for m in range(T):
                    take(kind, g, "at", m, adjTs[g.parity][:, m, :], whole(slot(kind, "at", m))).then_inc(read["at"], 1)

            def head_inputs(kind, o):
                take(kind, o, "x2T", 0, xT[:, :], whole(slot(kind, "x2T", 0))).then_inc(read["x2T"], 1)
                for k in range(2):
                    take(kind, o, "wh", k, wh[:, 4 * k:4 * k + 4, :],
                         quarters(slot(kind, "wh", k))[:, :, 0:D + 2 * H]).then_inc(read["wh"], 1)

            def sj_row(kind, o, h):
                if h >= 2:
                    act.wait_ge(step_made, o.count(H * T, (h - 1) * T))
                take(kind, o, "bc", h, sjrow[:, h % 2, :], whole(slot(kind, "bc", h))).then_inc(read["bc"], 1)

            def factors(o):
                act.wait_ge(exin_made, o.count(5, 5))
                act.activation(ex[:, :, :, :], exin[:, :, :, :], ACT.Exp).then_inc(ex_made, 1)

            def step_tile(o, h, t):
                n = h * T + t
                if n >= 2:
                    act.wait_ge(c_made, o.count(H * T, n - 1))
                if t == 0:
                    act.wait_ge(read["bc"], o.count(H, h + 1))
                act.activation(steps[:, n % 2, :], sjrow[:, h % 2, :], ACT.Relu, bias=steepsi[:, t, h:h + 1],
                               scale=STEEP).then_inc(step_made, 1)

            def exp_tile(kind, g, n):
                act.wait_ge(full["st"], g.count(T, n + 1))
                if g.turn is not None or g.base > 0 or n >= 2:
                    act.wait_ge(probs_used, g.count(T, n - 1))
                act.activation(probs[:, n % 2, :, :], slot(kind, "st", n)[:, :, :], ACT.Exp).then_inc(read["st"], 1)

            make_maskb(Graph(0))

            def step(kind, g):
                o = g.before()
                if kind != "last":
                    project(kind, g)
                if kind != "first":
                    head_inputs(kind, o)
                    sj_row(kind, o, 0)
                    sj_row(kind, o, 1)
                    factors(o)
                for n in range(T):
                    if kind != "last":
                        exp_tile(kind, g, n)
                    if kind != "first":
                        for j in (2 * n, 2 * n + 1):
                            step_tile(o, j // T, j % T)
                if kind != "first":
                    sj_row(kind, o, 2)
                    sj_row(kind, o, 3)
                    for j in range(2 * T):
                        step_tile(o, 2 + j // T, j % T)
                if kind == "first" or (kind == "full" and (g.turn is not None or g.base < NB - 1)):
                    make_maskb(Graph(g.base + 1, g.turn))
                if kind != "last":
                    take(kind, g, "agg1", 0, agg1T[:, :], whole(Z)).then_inc(read["agg1"], 1)
                if kind != "first":
                    take(kind, o, "agg3", 0, agg3T[:, :], whole(Z)).then_inc(read["agg3"], 1)

            program(act, step)

        @block.vector
        def _(dve):
            dve.wait_ge(ident_made, 2)
            dve.tensor_copy(ident16[:, :], identf[:, :]).then_inc(dve_init, 1)
            dve.tensor_copy(identb[:, :], identf[:, :]).then_inc(dve_init, 1)
            dve.wait_ge(consts_in, 16 * 10)
            heads = wext[:, 0:D].rearrange("p (h d) -> p h d", h=H)
            for n in range(2):
                dve.tensor_tensor(rest[:, n * D:(n + 1) * D].rearrange("p (h d) -> p h d", h=H), heads,
                                  abc[:, :, n, :], ALU.mult).then_inc(dve_init, 1)
            for n in range(2):
                dve.wait_ge(dve_init, 3 + n)
                dve.tensor_reduce(wext[:, D + n * H:D + (n + 1) * H],
                                  rest[:, n * D:(n + 1) * D].rearrange("p (h d) -> p h d", h=H), AX_X, ALU.add)\
                    .then_inc(dve_init, 1)
            dve.wait_ge(dve_init, 6)
            dve.tensor_copy(wdst[:, :, :], wext[:, D + H:D + 2 * H].unsqueeze(2).broadcast_to([P, H, P]))\
                .then_inc(dve_init, 1)

            def guards(kind, g):
                for t in range(T):
                    s = whole(slot(kind, "s", t))
                    dve.wait_ge(full["s"], g.count(T, t + 1))
                    dve.wait_ge(maskb_made, g.count(T, t + 1))
                    dve.nop(nofuse=True)
                    dve.tensor_tensor_reduce(out=s, in0=s, in1=maskb[:, t, :], scale=1.0, scalar=LOWEST,
                                             op0=ALU.add, op1=ALU.max, accum_out=smax[:, t:t + 1]).then_inc(read["s"], 1)
                    dve.wait_ge(read["s"], g.count(T, t + 1))
                    dve.tensor_scalar(negmax[:, t * P:(t + 1) * P], identb[:, :], smax[:, t:t + 1], -1.0,
                                      ALU.mult, ALU.mult).then_inc(negmax_made, 1)

            def guard_heads(o):
                si = wh[:, :, D:D + H]
                sj = wh[:, :, D + H:D + 2 * H]
                m = mall[:, :].unsqueeze(1).broadcast_to([P, T, H])
                dve.wait_ge(read["wh"], o.count(2, 2))
                dve.tensor_reduce(mloc[:, :], si.rearrange("p t h -> p h t"), AX_X, ALU.max).then_inc(mloc_made, 1)
                dve.tensor_scalar(steepsi[:, :, :], si, STEEP, None, ALU.mult)
                dve.wait_ge(mall_made, o.count(1, 1))
                dve.tensor_tensor(exin[:, 0, :, :], si, m, ALU.subtract).then_inc(exin_made, 1)
                dve.tensor_tensor(wsj[:, :, :], sj, m, ALU.add).then_inc(exin_made, 1)
                dve.wait_ge(exin_made, o.count(5, 1))
                dve.tensor_scalar(exin[:, 1, :, :], exin[:, 0, :, :], SLOPE2, None, ALU.mult).then_inc(exin_made, 1)
                dve.wait_ge(exin_made, o.count(5, 2))
                dve.tensor_scalar(exin[:, 2, :, :], wsj[:, :, :], 0.0, 1.0 - SLOPE2, ALU.min, ALU.mult)\
                    .then_inc(exin_made, 1)
                dve.tensor_scalar(exin[:, 3, :, :], wsj[:, :, :], 0.0, SLOPE2 - 1.0, ALU.max, ALU.mult)\
                    .then_inc(exin_made, 1)

            def split_values(o):
                v = vals[:, :, :, :].rearrange("p t h c -> p (t h) c")
                part = [vparts[:, :, :, n, :].rearrange("p t h c -> p (t h) c") for n in range(3)]
                dve.wait_ge(vals_made, o.count(4, 4))
                dve.tensor_copy(part[0], v).then_inc(vsplit, 1)
                dve.wait_ge(vsplit, o.count(4, 1))
                dve.tensor_tensor(v, v, part[0], ALU.subtract).then_inc(vsplit, 1)
                dve.wait_ge(vsplit, o.count(4, 2))
                dve.tensor_copy(part[1], v).then_inc(vsplit, 1)
                dve.wait_ge(vsplit, o.count(4, 3))
                dve.tensor_tensor(part[2], v, part[1], ALU.subtract).then_inc(vsplit, 1)

            def mins(o, h):
                if h >= 2:
                    dve.wait_ge(full["c"], o.count(2 * H, 2 * (h - 1)))
                for t in range(T):
                    n = h * T + t
                    dve.wait_ge(step_made, o.count(H * T, n + 1))
                    dve.tensor_tensor(cmat[:, h % 2, t, :], steps[:, n % 2, :], adjs[o.parity][:, t, :], ALU.min)\
                        .then_inc(c_made, 1)

            def context(g, k):
                zq = quarters(Z)
                dve.wait_ge(probs_used, g.count(T, 4 * k + 4))
                dve.reciprocal(rden[:, 4 * k:4 * k + 4], zq[:, :, D]).then_inc(rden_made, 1)
                dve.wait_ge(rden_made, g.count(2, k + 1))
                if k == 0:
                    dve.wait_ge(x0_biased, g.count(1, 1))
                for j in range(4):
                    t = 4 * k + j
                    ins = dve.scalar_tensor_tensor(x1[:, t, :], zq[:, j, 0:D], rden[:, t:t + 1], x0[:, t, :],
                                                   ALU.mult, ALU.add)
                ins.then_inc(y_made[0], 1)

            def norm_stats(layer, g, xn, k):
                dve.wait_ge(y_made[layer], g.count(2, k + 1))
                for t in range(4 * k, 4 * k + 4):
                    ins = dve.bn_stats(stats[:, t, :], xn[:, t, :])
                ins.then_inc(stats_made[layer], 1)
                dve.wait_ge(stats_made[layer], g.count(2, k + 1))
                dve.nop(nofuse=True)
                for t in range(4 * k, 4 * k + 4):
                    ins = dve.bn_aggr(meanvar[:, layer, t, :], stats[:, t, :])
                ins.then_inc(meanvar_made[layer], 1)

            def norm_apply(layer, g, xn, k):
                dve.wait_ge(rstd_made[layer], g.count(2, k + 1))
                for t in range(4 * k, 4 * k + 4):
                    ins = dve.tensor_scalar(xn[:, t, :], xn[:, t, :], meanvar[:, layer, t, 0:1], rstd[:, layer, t:t + 1],
                                            ALU.subtract, ALU.mult)
                ins.then_inc(normed[layer], 1)

            def split_half(parts, k, src, done, g, per, at):
                left = rest[:, :].rearrange("p (t d) -> p t d", d=D)
                ts = slice(4 * k, 4 * k + 4)
                dve.tensor_copy(parts[:, 0, ts, :], src).then_inc(done, 1)
                dve.wait_ge(done, g.count(per, at + 1))
                dve.tensor_tensor(left, src, parts[:, 0, ts, :], ALU.subtract).then_inc(done, 1)
                dve.wait_ge(done, g.count(per, at + 2))
                dve.tensor_copy(parts[:, 1, ts, :], left).then_inc(done, 1)
                dve.wait_ge(done, g.count(per, at + 3))
                dve.tensor_tensor(parts[:, 2, ts, :], left, parts[:, 1, ts, :], ALU.subtract).then_inc(done, 1)

            def split_x1(g, k):
                dve.wait_ge(normed[0], g.count(2, k + 1))
                split_half(parts1, k, x1[:, 4 * k:4 * k + 4, :], split1, g, 8, 4 * k)

            def split_x3(o, k):
                left = rest[:, :].rearrange("p (t d) -> p t d", d=D)
                dve.wait_ge(normed[2], o.count(2, k + 1))
                for j in range(4):
                    t = 4 * k + j
                    ins = dve.tensor_scalar(left[:, j, :], x3[:, t, :], dcol[o.parity][:, t:t + 1], None, ALU.mult)
                ins.then_inc(split3, 1)
                dve.wait_ge(split3, o.count(10, 5 * k + 1))
                split_half(parts3, k, left, split3, o, 10, 5 * k + 1)

            def sums_of_masks(kind, o):
                for k in range(2):
                    dve.wait_ge(full["mask"], o.count(2, k + 1))
                    dve.tensor_copy(msum[:, 4 * k:4 * k + 4, :], quarters(slot(kind, "mask", k))[:, :, 0:H * HW])\
                        .then_inc(read["mask"], 1)

            def sums_of_head(kind, o, h):
                for k in range(2):
                    n = 2 * h + k
                    if h >= 2 and k == 0:
                        dve.wait_ge(num_made, o.count(4 * H, 4 * (h - 1)))
                    dve.wait_ge(full["c"], o.count(2 * H, n + 1))
                    src = quarters(slot(kind, "c", n))[:, :, 0:3 * VW].rearrange("p t (s c) -> p t c s", s=3)
                    dve.tensor_reduce(csum[:, h % 2, 4 * k:4 * k + 4, :], src, AX_X, ALU.add).then_inc(read["c"], 1)

            def head_out(o, h):
                cols = slice(h * DH, (h + 1) * DH)
                dve.wait_ge(num_made, o.count(4 * H, 4 * h + 4))
                dve.reciprocal(rgat[:, :], num[:, :, DH]).then_inc(rgat_made, 1)
                dve.wait_ge(rgat_made, o.count(H, h + 1))
                dve.tensor_tensor(gatout[:, :, :], num[:, :, 0:DH], rgat[:, :].unsqueeze(2).broadcast_to([P, T, DH]),
                                  ALU.mult).then_inc(gat_made, 1)
                dve.wait_ge(gat_made, o.count(H, h + 1))
                if h == 0 and (o.turn is not None or o.base > 0):
                    dve.wait_ge(stored, o.count(16))
                for k in range(2):
                    ts = slice(4 * k, 4 * k + 4)
                    ins = dve.tensor_tensor(x3[:, ts, cols], gatout[:, ts, :], x2[:, ts, cols], ALU.add)
                    if h == H - 1:
                        ins.then_inc(y_made[2], 1)

            def layer1_out(kind, g, k):
                s = by_tile(slot(kind, "out1", k))
                half = x2[:, 4 * k:4 * k + 4, :]
                dve.wait_ge(full["out1"], g.count(2, k + 1))
                if k == 0:
                    dve.wait_ge(degrees, g.count(4, 4))
                for j in range(4):
                    t = 4 * k + j
                    ins = dve.scalar_tensor_tensor(x2[:, t, :], s[:, j, :], rrow[:, t:t + 1], b1_s[:, :], ALU.mult, ALU.add)
                ins.then_inc(read["out1"], 1)
                dve.wait_ge(read["out1"], g.count(2, k + 1))
                dve.scalar_tensor_tensor(half, half, SLOPE1, half, ALU.mult, ALU.max).then_inc(z1_made, 1)
                dve.wait_ge(z1_made, g.count(2, k + 1))
                dve.tensor_tensor(half, half, x1[:, 4 * k:4 * k + 4, :], ALU.add).then_inc(y_made[1], 1)

            def layer3_out(kind, o):
                s = by_tile(slot(kind, "out3", 0))
                dve.wait_ge(full["out3"], o.count(1, 1))
                for t in range(T):
                    ins = dve.scalar_tensor_tensor(x3[:, t, :], s[:, t, :], dcol[o.parity][:, t:t + 1], x3[:, t, :],
                                                   ALU.mult, ALU.add)
                    if t % 4 == 3:
                        ins.then_inc(y_made[3], 1)

            def step(kind, g):
                o = g.before()
                if kind != "last":
                    guards(kind, g)
                if kind != "first":
                    guard_heads(o)
                    split_values(o)
                    mins(o, 0)
                if kind != "last":
                    context(g, 0)
                    norm_stats(0, g, x1, 0)
                if kind != "first":
                    mins(o, 1)
                if kind != "last":
                    norm_apply(0, g, x1, 0)
                    context(g, 1)
                    norm_stats(0, g, x1, 1)
                    split_x1(g, 0)
                    norm_apply(0, g, x1, 1)
                    split_x1(g, 1)
                if kind != "first":
                    sums_of_masks(kind, o)
                    mins(o, 2)
                    sums_of_head(kind, o, 0)
                    mins(o, 3)
                    head_out(o, 0)
                    for h in range(1, H):
                        sums_of_head(kind, o, h)
                        head_out(o, h)
                    norm_stats(2, o, x3, 0)
                    norm_stats(2, o, x3, 1)
                    for k in range(2):
                        norm_apply(2, o, x3, k)
                        split_x3(o, k)
                if kind != "last":
                    layer1_out(kind, g, 0)
                    norm_stats(1, g, x2, 0)
                    layer1_out(kind, g, 1)
                    norm_stats(1, g, x2, 1)
                    norm_apply(1, g, x2, 0)
                    norm_apply(1, g, x2, 1)
                if kind != "first":
                    layer3_out(kind, o)
                    norm_stats(3, o, x3, 0)
                    norm_stats(3, o, x3, 1)
                    norm_apply(3, o, x3, 0)
                    norm_apply(3, o, x3, 1)

            program(dve, step)

        @block.tensor
        def _(pe):
            pe.wait_ge(ident_made, 2)
            pe.wait_ge(dve_init, 7)
            pe.wait_ge(pool_init, 5)
            pe.wait_ge(consts_in, 16 * 10)

            def claim(kind, g, name, k):
                n = ORDER[kind].index((name, k))
                if n >= SLOTS:
                    (was, j), of = ORDER[kind][n - SLOTS], g
                elif kind == "first":
                    return ring[n % SLOTS]
                elif g.turn is None and g.base == 1:
                    (was, j), of = ORDER["first"][n - SLOTS], g.before()
                else:
                    (was, j), of = ORDER["full"][n - SLOTS], g.before()
                if was in OLDER:
                    of = of.before()
                if was == "out3":
                    pe.wait_ge(y_made[3], of.count(2, 2))
                else:
                    pe.wait_ge(read[was], of.count(PER[was], j + 1))
                return ring[n % SLOTS]

            def transposes(kind, g, h, name, src):
                s = whole(claim(kind, h, name, 0))
                for t in range(T):
                    last = pe.transpose(s[:, t * P:(t + 1) * P], src[:, t, :], identf[:, :])
                last.then_inc(full[name], 1)

            def project(kind, g):
                pe.wait_ge(x_in, g.count(16, 16))
                transposes(kind, g, g, "xT", x0)
                pe.wait_ge(read["xT"], g.count(1, 1))
                for name, w in (("q", wq_s), ("k", wk_s)):
                    s = claim(kind, g, name, 0)
                    for c in range(2):
                        last = pe.matmul(s[:, c, :], w[:, :], xT[:, c * 512:(c + 1) * 512], start=True, stop=True)
                    last.then_inc(full[name], 1)
                s = by_tile(claim(kind, g, "v", 0))
                for t in range(T):
                    last = pe.matmul(s[:, t, :], xT[:, t * P:(t + 1) * P], wv_s[:, :], start=True, stop=True)
                last.then_inc(full["v"], 1)

            def transpose_adj(kind, g):
                pe.wait_ge(adj_in[g.parity], g.count_own(16, 16))
                for m in range(T):
                    s = by_tile(claim(kind, g, "at", m))
                    for t in range(T):
                        last = pe.matmul(s[:, t, :], adjs[g.parity][:, t, m * P:(m + 1) * P], ident16[:, :],
                                         start=True, stop=True)
                    last.then_inc(full["at"], 1)

            def guard_scores(kind, g, t):
                s = claim(kind, g, "s", t)
                if t == 0:
                    pe.wait_ge(read["q"], g.count(1, 1))
                    pe.wait_ge(read["k"], g.count(1, 1))
                for c in range(2):
                    last = pe.matmul(s[:, c, :], qb[:, t * P:(t + 1) * P], kb[:, c * 512:(c + 1) * 512],
                                     start=True, stop=True)
                last.then_inc(full["s"], 1)

            def head_inputs(kind, g, name, k):
                o = g.before()
                if name == "x2T":
                    pe.wait_ge(normed[1], o.count(2, 2))
                    transposes(kind, o, g, "x2T", x2)
                elif name == "wh":
                    s = quarters(claim(kind, g, "wh", k))
                    if k == 0:
                        pe.wait_ge(read["x2T"], o.count(1, 1))
                    for j in range(4):
                        t = 4 * k + j
                        last = pe.matmul(s[:, j, 0:D + 2 * H], xT[:, t * P:(t + 1) * P], wext[:, :], start=True, stop=True)
                    last.then_inc(full["wh"], 1)
                else:
                    s = claim(kind, g, "bc", k)
                    for c in range(2):
                        last = pe.matmul(s[:, c, :], wdst[:, k, :], xT[:, c * 512:(c + 1) * 512], start=True, stop=True)
                    last.then_inc(full["bc"], 1)

            def scores(kind, g, n):
                c = n // 4
                s = claim(kind, g, "st", n)
                for j in range(2):
                    kt = 2 * (n % 4) + j
                    pe.matmul(s[:, j, :], kT[:, kt * P:(kt + 1) * P], qT[:, c * 512:(c + 1) * 512],
                              start=True, stop=False)
                    for q in range(4):
                        pe.matmul(s[:, j, q * P:(q + 1) * P], maskb[:, 4 * c + q, kt * P:(kt + 1) * P],
                                  ident16[:, :], start=False, stop=False, skip_group_check=True)
                    if n % 4 == 0 and j == 0:
                        pe.wait_ge(negmax_made, g.count(T, 4 * c + 4))
                    last = pe.matmul(s[:, j, :], onesb[:, :], negmax[:, c * 512:(c + 1) * 512],
                                     start=False, stop=True)
                last.then_inc(full["st"], 1)

            def context(g, n):
                c = n // 4
                zq = quarters(Z)
                if n == 0:
                    pe.wait_ge(read["v"], g.count(1, 1))
                    if g.turn is not None or g.base > 1:
                        pe.wait_ge(read["agg3"], g.before(2).count(1, 1))
                    if g.turn is not None or g.base > 0:
                        pe.wait_ge(read["agg1"], g.count(1))
                elif n == 4:
                    pe.wait_ge(y_made[0], g.count(2, 1))
                pe.wait_ge(read["st"], g.count(T, n + 1))
                for j in range(2):
                    kt = 2 * (n % 4) + j
                    for q in range(4):
                        last = pe.matmul(zq[:, q, 0:D + 1], probs[:, n % 2, j, q * P:(q + 1) * P], vv[:, kt, :],
                                         start=kt == 0 and q % 2 == 0, stop=kt == T - 1, skip_group_check=True)
                last.then_inc(probs_used, 1)

            def mask_sums(kind, g, k):
                o = g.before()
                s = quarters(claim(kind, g, "mask", k))
                if k == 0:
                    pe.wait_ge(vsplit, o.count(4, 4))
                for j in range(4):
                    jt = 4 * k + j
                    for t in range(T):
                        for part in range(3):
                            last = pe.matmul(s[:, j, 0:H * HW], adjs[o.parity][:, t, jt * P:(jt + 1) * P],
                                             vparts[:, t, :, part, HW:VW], start=t == 0 and part == 0,
                                             stop=t == T - 1 and part == 2)
                last.then_inc(full["mask"], 1)

            def head_sums(kind, g, n):
                o = g.before()
                h = n // 2
                s = quarters(claim(kind, g, "c", n))
                for j in range(4):
                    jt = 4 * (n % 2) + j
                    for t in range(T):
                        if n % 2 == 0 and j == 0:
                            pe.wait_ge(c_made, o.count(H * T, h * T + t + 1))
                        last = pe.matmul(s[:, j, 0:3 * VW], cmat[:, h % 2, t, jt * P:(jt + 1) * P],
                                         vparts[:, t, h, :, :], start=t == 0, stop=t == T - 1)
                last.then_inc(full["c"], 1)

            def aggregate(name, g, parts, mat):
                for t in range(T):
                    for part in range(3):
                        for c in range(2):
                            last = pe.matmul(Z[:, c, :], parts[:, part, t, :], mat[:, t, c * 512:(c + 1) * 512],
                                             start=t == 0 and part == 0, stop=t == T - 1 and part == 2)
                last.then_inc(full[name], 1)

            def layer1(kind, g):
                pe.wait_ge(split1, g.count(8, 8))
                pe.wait_ge(y_made[0], g.count(2, 2))
                pe.wait_ge(read["at"], g.count(T, T))
                aggregate("agg1", g, parts1, adjTs[g.parity])
                pe.wait_ge(read["agg1"], g.count(1, 1))
                for k in range(2):
                    s = by_tile(claim(kind, g, "out1", k))
                    for j in range(4):
                        t = 4 * k + j
                        last = pe.matmul(s[:, j, :], agg1T[:, t * P:(t + 1) * P], w1_s[:, :], start=True, stop=True)
                    last.then_inc(full["out1"], 1)

            def layer3(kind, g):
                o = g.before()
                pe.wait_ge(split3, o.count(10, 10))
                pe.wait_ge(diag_added, o.count(1, 1))
                if kind == "last":
                    pe.wait_ge(read["agg1"], o.count(1, 1))
                aggregate("agg3", o, parts3, adjTs[o.parity])
                pe.wait_ge(read["agg3"], o.count(1, 1))
                s = by_tile(claim(kind, g, "out3", 0))
                for t in range(T):
                    last = pe.matmul(s[:, t, :], agg3T[:, t * P:(t + 1) * P], b3_s[:, :], start=True, stop=True)
                last.then_inc(full["out3"], 1)

            def step(kind, g):
                if kind != "last":
                    project(kind, g)
                    transpose_adj(kind, g)
                pairs = {"first": score, "full": mixed, "last": heads_up}[kind]
                for name, k in pairs:
                    if name == "s":
                        guard_scores(kind, g, k)
                    else:
                        head_inputs(kind, g, name, k)
                if kind != "last":
                    scores(kind, g, 0)
                    for n in range(1, T):
                        scores(kind, g, n)
                        context(g, n - 1)
                    context(g, T - 1)
                if kind != "first":
                    head_inputs(kind, g, "bc", 2)
                    head_inputs(kind, g, "bc", 3)
                    mask_sums(kind, g, 0)
                    mask_sums(kind, g, 1)
                    for n in range(2 * H):
                        head_sums(kind, g, n)
                if kind != "last":
                    layer1(kind, g)
                if kind != "first":
                    layer3(kind, g)

            program(pe, step)


_INS = ['x', 'adj', 'WqT', 'bq', 'WkT', 'WvT', 'bv', 'W1T', 'b1', 'W2', 'a2', 'B3']


def kernel(**inputs):
    import numpy as _np
    import concourse.bacc as _bacc
    from concourse import mybir as _mybir
    from concourse.bass_utils import run_bass_kernel_spmd as _run

    given = {
        'x': inputs['x'], 'adj': inputs['adj'],
        'WqT': _np.asarray(inputs['L0_gnn_Wq']).T, 'bq': inputs['L0_gnn_bq'],
        'WkT': _np.asarray(inputs['L0_gnn_Wk']).T, 'WvT': _np.asarray(inputs['L0_gnn_Wv']).T,
        'bv': inputs['L0_gnn_bv'],
        'W1T': _np.asarray(inputs['L1_gnn_W']).T, 'b1': inputs['L1_gnn_b'],
        'W2': inputs['L2_gnn_W'], 'a2': inputs['L2_gnn_a'], 'B3': inputs['L3_gnn_B'],
    }
    nc = _bacc.Bacc("TRN2", target_bir_lowering=False, num_devices=1)
    arrays, args = {}, []
    for name in _INS:
        a = _np.ascontiguousarray(given[name])
        arrays[f"in_{name}_dram"] = a
        args.append(nc.dram_tensor(f"in_{name}_dram", a.shape, _mybir.dt.from_np(a.dtype), kind="ExternalInput").ap())
    shape = tuple(inputs['x'].shape)
    args.append(nc.dram_tensor("out_0_dram", shape, _mybir.dt.float32, kind="ExternalOutput").ap())
    gnn_kernel(nc, *args)
    r = _run(nc, [arrays], core_ids=[0])
    return r.results[0]["out_0_dram"]
```

```python
from contextlib import ExitStack

import concourse.bass as bass
from concourse import mybir

F32 = mybir.dt.float32
F16 = mybir.dt.float16
BF16 = mybir.dt.bfloat16
ALU = mybir.AluOpType
ACT = mybir.ActivationFunctionType
AX_X = mybir.AxisListType.X
RMAX = bass.bass_isa.ReduceOp.max

P = 128
EPS = 1e-5
NEG = 10000.0
STEEP = 1e20
SLOPE1 = 0.01
SLOPE2 = 0.2
LOWEST = -3.0e38
TO_EIGHTS = 1.5 * 2.0 ** 26


class Graph:

    def __init__(self, base, turn=None):
        self.base, self.turn = base, turn
        self.parity = base % 2

    def before(self, n=1):
        return Graph(self.base - n, self.turn)

    def count(self, per, k=0):
        n = self.base * per + k
        return n if self.turn is None else self.turn * (2 * per) + n

    def count_own(self, per, k):
        n = (self.base // 2) * per + k
        return n if self.turn is None else self.turn * per + n


def gnn_kernel(nc, x, adj, Wq, bq, Wk, WvT, bv, W1T, b1, W2, a2, B3, out):
    NB, N, D = x.shape
    T = N // P
    H = a2.shape[0]
    DH = D // H
    SCALE = float(D) ** -0.5
    VW = 2 * DH + 2
    HW = DH + 1
    assert D == P and T == 8 and NB % 2 == 0

    x_v = x.rearrange("b (t p) d -> b p t d", p=P)
    adj_v = adj.rearrange("b (t p) m -> b p t m", p=P)
    out_v = out.rearrange("b (t p) d -> b p t d", p=P)
    sj_dram = nc.dram_tensor("sj_rows", (H, N), F32).ap()

    project = [("xT", 0), ("q", 0), ("v", 0)]
    at, s_groups = [("at", m) for m in range(T)], [("s", t) for t in range(T)]
    heads_up = [("x2T", 0), ("wh", 0), ("wh", 1), ("sj", 0)]
    mixed = (at[0:4] + [s_groups[0], at[4], s_groups[1], at[5], heads_up[0], s_groups[2], at[6], heads_up[1],
                        s_groups[3], at[7], heads_up[2], s_groups[4], heads_up[3]] + s_groups[5:])
    soft = [("st", g) for g in range(T)]
    gat = [("mask", 0), ("mask", 1)] + [("c", g) for g in range(2 * H)]
    ORDER = {
        "first": project + at + s_groups + soft + [("out1", 0), ("out1", 1)],
        "full": project + mixed + soft + gat + [("out1", 0), ("out1", 1), ("out3", 0), ("out3", 1)],
        "last": heads_up + gat + [("out3", 0), ("out3", 1)],
    }
    SLOTS = 3
    assert len(ORDER["full"]) % SLOTS == 0
    SHIFT = {"first": -len(ORDER["first"]) % SLOTS, "full": 0, "last": 0}
    OLDER = ("x2T", "wh", "sj", "mask", "c", "out3")

    ctx = ExitStack()
    with ctx:
        def sb(name, shape, dt):
            return ctx.enter_context(nc.sbuf_tensor(name, shape, dt))

        def sem(name):
            return ctx.enter_context(nc.semaphore(name))

        adjs = [sb(f"adj{p}", [P, T, N], F16) for p in range(2)]
        adjTs = [sb(f"adjT{p}", [P, T, N], F16) for p in range(2)]
        maskb = sb("maskb", [P, T, N], F16)
        cmat = sb("cmat", [P, 2, T, N], F16)
        C_OF = [cmat[:, 0, :, :], cmat[:, 1, :, :], maskb[:, :, :], cmat[:, 0, :, :]]
        vals = cmat[:, 1, :, :].rearrange("p t n -> p (t n)")[:, 0:2 * T * H * VW].bitcast(F32)\
            .rearrange("p (t h c) -> p t h c", h=H, c=VW)
        probs = sb("probs", [P, 2, 2, 512], F32)
        msum = probs[:, :, :, :].rearrange("p a b c -> p (a b c)")[:, 0:T * H * HW]\
            .rearrange("p (t c) -> p t c", t=T)
        x0 = sb("x0", [P, T, D], F32)
        x1 = sb("x1", [P, T, D], F32)
        x2 = sb("x2", [P, T, D], F32)
        x3 = sb("x3", [P, T, D], F32)
        parts1 = sb("parts1", [P, 3, T, D], BF16)
        xT = sb("xT", [P, N], F32)
        qT = sb("qT", [P, N], F32)
        x2T = sb("x2T", [P, N], F32)
        agg1T, agg3T = qT, x2T
        vparts = sb("vparts", [P, T, H, 3, VW], BF16)
        flat = vparts[:, :, :, :, :].rearrange("p t h s c -> p (t h s c)")
        qb, xb = flat[:, 0:N], flat[:, N:2 * N]
        parts3 = flat[:, 0:3 * N].rearrange("p (s t d) -> p s t d", s=3, d=D)
        vv = sb("vv", [P, T, D + 1], F32)
        wh = sb("wh", [P, T, D + 2 * H], F32)
        sjrow = sb("sjrow", [P, 2, N], F32)
        steps = sb("steps", [P, 2, N], BF16)
        csum = sb("csum", [P, 2, T, VW], F32)
        abc = csum[:, 0, :, :].rearrange("p t c -> p (t c)")[:, 0:2 * D]\
            .rearrange("p (h s d) -> p h s d", h=H, s=2)
        sjT = csum[0:H, :, :, :].rearrange("p a t c -> p (a t c)")[:, 0:N]
        num = sb("num", [P, T, HW], F32)
        num2 = sb("num2", [P, T, HW], F32)
        gatout = sb("gatout", [P, T, DH], F32)
        rest = sb("rest", [P, 4 * D], F32)

        identf = sb("identf", [P, P], F32)
        ident16 = sb("ident16", [P, P], F16)
        wq_s = sb("wq_s", [P, D], F32)
        wk_s = sb("wk_s", [P, D], F32)
        wqk = sb("wqk", [P, D], F32)
        wv_s = sb("wv_s", [P, D], F32)
        w1_s = sb("w1_s", [P, D], F32)
        b3_s = sb("b3_s", [P, D], F32)
        wext = sb("wext", [P, D + 2 * H], F32)
        bv_s = sb("bv_s", [P, D], F32)
        b1_s = sb("b1_s", [P, D], F32)
        bqcol = sb("bqcol", [P, 2], F32)
        powers = sb("powers", [P, T, 2], F32)

        rowacc = sb("rowacc", [P, T], F32)
        degree = sb("degree", [P, T], F32)
        rrow = sb("rrow", [P, T], F32)
        dcol = [sb(f"dcol{p}", [P, T], F32) for p in range(2)]
        smax = sb("smax", [P, T], F32)
        guard = sb("guard", [P, T], F32)
        rden = sb("rden", [P, T], F32)
        rgat = sb("rgat", [P, T], F32)
        mloc = sb("mloc", [P, H], F32)
        mall = sb("mall", [P, H], F32)
        wsj = sb("wsj", [P, T, H], F32)
        exin = sb("exin", [P, 4, T, H], F32)
        ex = sb("ex", [P, 4, T, H], F32)
        steepsi = sb("steepsi", [P, T, H], F32)
        stats = sb("stats", [P, T, 6], F32)
        meanvar = sb("meanvar", [P, 4, T, 2], F32)
        vareps = sb("vareps", [P, 4, T], F32)
        rstd = sb("rstd", [P, 4, T], F32)

        ring = [ctx.enter_context(nc.psum_tensor(f"ring{s}", [P, 2, 512], F32)) for s in range(SLOTS)]
        Z = ctx.enter_context(nc.psum_tensor("Z", [P, 2, 512], F32))

        consts_in = sem("consts_in")
        x_in = sem("x_in")
        adj_in = [sem("adj_in0"), sem("adj_in1")]
        stored = sem("stored")
        ident_made = sem("ident_made")
        dve_init = sem("dve_init")
        pool_init = sem("pool_init")
        act_init = sem("act_init")
        wqk_full = sem("wqk_full")
        full = {n: sem(f"{n}_full") for n in
                ("xT", "q", "v", "at", "s", "st", "agg1", "out1", "x2T", "wh", "sj", "mask", "c", "agg3", "out3")}
        read = {n: sem(f"{n}_read") for n in full if n != "out3"}
        PER = {"xT": 1, "q": 1, "v": 1, "at": T, "s": T, "st": T, "agg1": 1, "out1": 2,
               "x2T": 1, "wh": 2, "sj": 1, "mask": 2, "c": 2 * H, "agg3": 1, "out3": 2}
        x0_biased = sem("x0_biased")
        maskb_made = sem("maskb_made")
        rowsums = sem("rowsums")
        degrees = sem("degrees")
        guard_made = sem("guard_made")
        guarded = sem("guarded")
        sj_kept = sem("sj_kept")
        sj_in = [sem("sj_in0"), sem("sj_in1")]
        probs_used = sem("probs_used")
        rden_made = sem("rden_made")
        y_made = [sem(f"y_made{n}") for n in range(4)]
        stats_made = [sem(f"stats_made{n}") for n in range(4)]
        meanvar_made = [sem(f"meanvar_made{n}") for n in range(4)]
        vareps_made = [sem(f"vareps_made{n}") for n in range(4)]
        rstd_made = [sem(f"rstd_made{n}") for n in range(4)]
        normed = [sem(f"normed{n}") for n in range(4)]
        split1 = sem("split1")
        split3 = sem("split3")
        z1_made = sem("z1_made")
        mloc_made = sem("mloc_made")
        mall_made = sem("mall_made")
        exin_made = sem("exin_made")
        ex_made = sem("ex_made")
        vals_made = sem("vals_made")
        vsplit = sem("vsplit")
        step_made = sem("step_made")
        c_made = sem("c_made")
        num_made = sem("num_made")
        rgat_made = sem("rgat_made")
        gat_made = sem("gat_made")
        diag_added = sem("diag_added")

        CONSTS = 12
        block = ctx.enter_context(nc.Block())

        def slot(kind, name, k):
            return ring[(ORDER[kind].index((name, k)) + SHIFT[kind]) % SLOTS]

        def quarter(slot_, n):
            return slot_[:, n // 2, (n % 2) * 256:(n % 2) * 256 + 256]

        def quarters(slot_):
            return slot_[:, :, :].rearrange("p b (a c) -> p (b a) c", a=2)

        def whole(slot_):
            return slot_[:, :, :].rearrange("p b c -> p (b c)")

        def by_tile(slot_):
            return whole(slot_).rearrange("p (t c) -> p t c", c=P)

        def program(engine, step):
            step("first", Graph(0))
            step("full", Graph(1))
            with engine.Fori(0, NB // 2 - 2) as turn:
                step("full", Graph(2, turn))
                step("full", Graph(3, turn))
            step("full", Graph(NB - 2))
            step("full", Graph(NB - 1))
            step("last", Graph(NB))

        @block.sync
        def _(sp):
            for dst, src in ((wq_s, Wq), (wk_s, Wk), (wv_s, WvT), (w1_s, W1T), (b3_s, B3)):
                sp.dma_start(dst[:, :], src).then_inc(consts_in, 16)
            sp.dma_start(wext[:, 0:D], W2).then_inc(consts_in, 16)
            sp.dma_start(bqcol[:, 0:1], bq.rearrange("(p a) -> p a", a=1)).then_inc(consts_in, 16)
            for dst, src in ((bv_s, bv), (b1_s, b1)):
                sp.dma_start(dst[:, :], src.rearrange("(a d) -> a d", a=1).broadcast_to([P, D])).then_inc(consts_in, 16)
            sp.dma_start(csum[:, 0, :, :].rearrange("p t c -> p (t c)")[:, 0:2 * D],
                         a2.rearrange("(a h) c -> a (h c)", a=1).broadcast_to([P, 2 * D])).then_inc(consts_in, 16)
            sp.dma_start(x0[:, :, :], x_v[0]).then_inc(x_in, 16)

            def number(g):
                return g.base if g.turn is None else g.turn * 2 + g.base

            def spread_sj(o):
                sp.wait_ge(read["sj"], o.count(1, 1))
                sp.dma_start(sj_dram, sjT).then_inc(sj_kept, 16)
                sp.wait_ge(sj_kept, o.count(16, 16))
                for h in range(H):
                    if h >= 2:
                        sp.wait_ge(step_made, o.count(H * T, (h - 1) * T))
                    sp.dma_start(sjrow[:, h % 2, :], sj_dram[h:h + 1, :].broadcast_to([P, N])).then_inc(sj_in[h % 2], 16)

            def step(kind, g):
                o = g.before()
                if kind != "first":
                    spread_sj(o)
                if kind != "last" and (g.turn is not None or g.base < NB - 1):
                    sp.wait_ge(y_made[0], g.count(2, 2))
                    sp.dma_start(x0[:, :, :], x_v[number(Graph(g.base + 1, g.turn))]).then_inc(x_in, 16)
                if kind != "first":
                    sp.wait_ge(normed[3], o.count(2, 2))
                    sp.dma_start(out_v[number(o)], x3[:, :, :]).then_inc(stored, 16)

            program(sp, step)
            sp.wait_ge(stored, 16 * NB)

        @block.gpsimd
        def _(pool):
            def load_adj(g):
                n = g.base if g.turn is None else g.turn * 2 + g.base
                pool.dma_start(adjs[g.parity][:, :, :], adj_v[n]).then_inc(adj_in[g.parity], 16)

            load_adj(Graph(0))
            pool.memset(identf[:, :], 0.0).then_inc(ident_made, 1)
            pool.wait_ge(ident_made, 1)
            pool.affine_select(out=identf[:, :], in_=identf[:, :], compare_op=ALU.not_equal, fill=1.0,
                               base=0, pattern=[[-1, P]], channel_multiplier=1).then_inc(ident_made, 1)
            load_adj(Graph(1))
            pool.memset(powers[:, :, 0], -0.5).then_inc(pool_init, 1)
            pool.memset(powers[:, :, 1], -1.0).then_inc(pool_init, 1)
            pool.memset(vv[:, :, D:D + 1], 1.0).then_inc(pool_init, 1)
            pool.wait_ge(pool_init, 3)
            pool.wait_ge(consts_in, 16 * 10)

            def bias_x0(g):
                pool.wait_ge(full["xT"], g.count(1, 1))
                pool.tensor_tensor(x0[:, :, :], x0[:, :, :], bv_s[:, :].unsqueeze(1).broadcast_to([P, T, D]),
                                   ALU.add).then_inc(x0_biased, 1)

            def degree_of(g):
                pool.wait_ge(rowsums, g.count(T, T))
                pool.nop(nofuse=True)
                pool.tensor_scalar(degree[:, :], rowacc[:, :], 1.0, None, ALU.add).then_inc(degrees, 1)
                pool.tensor_tensor(rrow[:, :], rowacc[:, :], powers[:, :, 1], ALU.pow).then_inc(degrees, 1)
                pool.wait_ge(degrees, g.count(3, 1))
                pool.tensor_tensor(dcol[g.parity][:, :], degree[:, :], powers[:, :, 0], ALU.pow).then_inc(degrees, 1)

            def rstd_of(layer, g):
                for k in range(2):
                    ts = slice(4 * k, 4 * k + 4)
                    pool.wait_ge(meanvar_made[layer], g.count(2, k + 1))
                    pool.nop(nofuse=True)
                    pool.tensor_scalar(vareps[:, layer, ts], meanvar[:, layer, ts, 1], EPS, None, ALU.add)\
                        .then_inc(vareps_made[layer], 1)
                    pool.wait_ge(vareps_made[layer], g.count(2, k + 1))
                    pool.tensor_tensor(rstd[:, layer, ts], vareps[:, layer, ts], powers[:, 0:4, 0], ALU.pow)\
                        .then_inc(rstd_made[layer], 1)

            def values_of(o):
                pool.wait_ge(mloc_made, o.count(1, 1))
                pool.nop(nofuse=True)
                pool.partition_all_reduce(mall[:, :], mloc[:, :], P, RMAX).then_inc(mall_made, 1)
                pool.wait_ge(ex_made, o.count(1, 1))
                heads = wh[:, :, 0:D].rearrange("p t (h d) -> p t h d", h=H)
                for n in range(2):
                    at = n * HW
                    pool.tensor_tensor(vals[:, :, :, at:at + DH], heads,
                                       ex[:, n, :, :].unsqueeze(3).broadcast_to([P, T, H, DH]), ALU.mult)\
                        .then_inc(vals_made, 1)
                    pool.tensor_copy(vals[:, :, :, at + DH], ex[:, n, :, :]).then_inc(vals_made, 1)

            def combine_heads(o):
                for h in range(H):
                    pool.wait_ge(read["c"], o.count(2 * H, 2 * h + 2))
                    if h == 0:
                        pool.wait_ge(read["mask"], o.count(2, 2))
                    else:
                        pool.wait_ge(rgat_made, o.count(H, h))
                        pool.wait_ge(gat_made, o.count(H, h))
                    cs = csum[:, h % 2, :, :]
                    f = [ex[:, 2 + n, :, h].unsqueeze(2).broadcast_to([P, T, HW]) for n in range(2)]
                    pool.tensor_tensor(num[:, :, :], msum[:, :, h * HW:(h + 1) * HW], cs[:, :, HW:VW], ALU.subtract)\
                        .then_inc(num_made, 1)
                    pool.tensor_tensor(num2[:, :, :], cs[:, :, 0:HW], f[0], ALU.mult).then_inc(num_made, 1)
                    pool.wait_ge(num_made, o.count(4 * H, 4 * h + 1))
                    pool.tensor_tensor(num[:, :, :], num[:, :, :], f[1], ALU.mult).then_inc(num_made, 1)
                    pool.wait_ge(num_made, o.count(4 * H, 4 * h + 3))
                    pool.tensor_tensor(num[:, :, :], num[:, :, :], num2[:, :, :], ALU.add).then_inc(num_made, 1)

            def add_diagonal(g):
                pool.wait_ge(full["agg1"], g.count(1, 1))
                for t in range(T):
                    d = adjTs[g.parity][:, t, t * P:(t + 1) * P]
                    ins = pool.tensor_tensor(d, d, ident16[:, :], ALU.add)
                ins.then_inc(diag_added, 1)

            def step(kind, g):
                o = g.before()
                if kind != "last":
                    bias_x0(g)
                if kind != "first":
                    values_of(o)
                if kind != "last":
                    rstd_of(0, g)
                if kind != "first":
                    combine_heads(o)
                    rstd_of(2, o)
                    if kind == "full" and (g.turn is not None or g.base < NB - 1):
                        pool.wait_ge(read["c"], o.count(2 * H, 2 * H))
                        load_adj(Graph(g.base + 1, g.turn))
                if kind != "last":
                    degree_of(g)
                    add_diagonal(g)
                    rstd_of(1, g)
                if kind != "first":
                    rstd_of(3, o)

            program(pool, step)

        @block.scalar
        def _(act):
            act.wait_ge(wqk_full, 1)
            act.activation(wqk[:, :], ring[0][:, 0, 0:D], ACT.Copy)
            act.activation(bqcol[:, 1:2], ring[0][:, 1, 0:1], ACT.Copy, scale=SCALE).then_inc(act_init, 1)
            act.wait_ge(act_init, 1)

            def sum_rows(g):
                if g.turn is not None or g.base > 0:
                    act.wait_ge(c_made, g.count(H * T))
                    act.wait_ge(degrees, g.count(3))
                for t in range(T):
                    if t >= 2:
                        act.wait_ge(rowsums, g.count(T, t - 1))
                    act.activation(steps[:, t % 2, :], adjs[g.parity][:, t, :], ACT.Copy,
                                   accum_out=rowacc[:, t:t + 1]).then_inc(rowsums, 1)

            def take(kind, g, name, k, dst, src):
                act.wait_ge(full[name], g.count(PER[name], k + 1))
                return act.activation(dst, src, ACT.Copy)

            def project(kind, g):
                s = whole(slot(kind, "xT", 0))
                take(kind, g, "xT", 0, xT[:, :], s)
                act.activation(xb, s, ACT.Copy).then_inc(read["xT"], 1)
                s = whole(slot(kind, "q", 0))
                act.wait_ge(full["q"], g.count(1, 1))
                act.activation(qT[:, :], s, ACT.Identity, bias=bqcol[:, 1:2], scale=SCALE)
                act.activation(qb, s, ACT.Identity, bias=bqcol[:, 1:2], scale=SCALE).then_inc(read["q"], 1)
                take(kind, g, "v", 0, vv[:, :, 0:D], by_tile(slot(kind, "v", 0))).then_inc(read["v"], 1)

            def take_group(kind, g, name, k):
                o = g.before()
                src = slot(kind, name, k)
                if name == "at":
                    take(kind, g, name, k, adjTs[g.parity][:, k, :], whole(src)).then_inc(read[name], 1)
                elif name == "x2T":
                    take(kind, o, name, k, x2T[:, :], whole(src)).then_inc(read[name], 1)
                elif name == "wh":
                    take(kind, o, name, k, wh[:, 4 * k:4 * k + 4, :], quarters(src)[:, :, 0:D + 2 * H])\
                        .then_inc(read[name], 1)
                elif name == "sj":
                    take(kind, o, name, k, sjT, whole(src)[0:H, :]).then_inc(read[name], 1)

            def factors(o):
                act.wait_ge(exin_made, o.count(5, 5))
                act.activation(ex[:, :, :, :], exin[:, :, :, :], ACT.Exp).then_inc(ex_made, 1)

            def step_tile(o, h, t):
                n = h * T + t
                if n >= 2:
                    act.wait_ge(c_made, o.count(H * T, n - 1))
                if t == 0:
                    act.wait_ge(sj_in[h % 2], o.count(32, 16 * (h // 2) + 16))
                act.activation(steps[:, n % 2, :], sjrow[:, h % 2, :], ACT.Relu, bias=steepsi[:, t, h:h + 1],
                               scale=STEEP).then_inc(step_made, 1)

            def exp_tile(kind, g, n):
                act.wait_ge(full["st"], g.count(T, n + 1))
                if g.turn is not None or g.base > 0 or n >= 2:
                    act.wait_ge(probs_used, g.count(T, n - 1))
                act.activation(probs[:, n % 2, :, :], slot(kind, "st", n)[:, :, :], ACT.Exp).then_inc(read["st"], 1)

            def step(kind, g):
                o = g.before()
                if kind != "last":
                    project(kind, g)
                for name, k in {"first": at, "full": mixed, "last": heads_up}[kind]:
                    take_group(kind, g, name, k)
                if kind != "first":
                    factors(o)
                for n in range(T):
                    if kind != "last":
                        exp_tile(kind, g, n)
                    if kind != "first":
                        for j in (2 * n, 2 * n + 1):
                            step_tile(o, j // T, j % T)
                if kind != "first":
                    for j in range(2 * T):
                        step_tile(o, 2 + j // T, j % T)
                if kind != "last":
                    sum_rows(g)
                    take(kind, g, "agg1", 0, agg1T[:, :], whole(Z)).then_inc(read["agg1"], 1)
                if kind != "first":
                    take(kind, o, "agg3", 0, agg3T[:, :], whole(Z)).then_inc(read["agg3"], 1)

            program(act, step)

        @block.vector
        def _(dve):
            dve.wait_ge(ident_made, 2)
            dve.tensor_copy(ident16[:, :], identf[:, :]).then_inc(dve_init, 1)
            dve.wait_ge(consts_in, 16 * 10)
            heads = wext[:, 0:D].rearrange("p (h d) -> p h d", h=H)
            for n in range(2):
                dve.tensor_tensor(rest[:, n * D:(n + 1) * D].rearrange("p (h d) -> p h d", h=H), heads,
                                  abc[:, :, n, :], ALU.mult).then_inc(dve_init, 1)
            for n in range(2):
                dve.wait_ge(dve_init, 2 + n)
                dve.tensor_reduce(wext[:, D + n * H:D + (n + 1) * H],
                                  rest[:, n * D:(n + 1) * D].rearrange("p (h d) -> p h d", h=H), AX_X, ALU.add)\
                    .then_inc(dve_init, 1)
            dve.wait_ge(dve_init, 5)

            def make_maskb(g):
                dve.wait_ge(adj_in[g.parity], g.count_own(16, 16))
                if g.turn is not None or g.base > 0:
                    dve.wait_ge(full["st"], g.count(T))
                if g.turn is not None or g.base > 1:
                    dve.wait_ge(full["c"], g.before().count(2 * H, -2))
                for t in range(T):
                    dve.tensor_scalar(maskb[:, t, :], adjs[g.parity][:, t, :], NEG, -NEG, ALU.mult, ALU.add)\
                        .then_inc(maskb_made, 1)

            def guards(kind, g):
                for t in range(T):
                    s = whole(slot(kind, "s", t))
                    dve.wait_ge(full["s"], g.count(T, t + 1))
                    dve.wait_ge(maskb_made, g.count(T, t + 1))
                    dve.nop(nofuse=True)
                    dve.tensor_tensor_reduce(out=s, in0=s, in1=maskb[:, t, :], scale=1.0, scalar=LOWEST,
                                             op0=ALU.add, op1=ALU.max, accum_out=smax[:, t:t + 1]).then_inc(read["s"], 1)
                    dve.wait_ge(read["s"], g.count(T, t + 1))
                    dve.tensor_scalar(guard[:, t:t + 1], smax[:, t:t + 1], TO_EIGHTS, -TO_EIGHTS, ALU.add, ALU.add)\
                        .then_inc(guard_made, 1)
                    dve.wait_ge(guard_made, g.count(T, t + 1))
                    dve.tensor_scalar(maskb[:, t, :], maskb[:, t, :], guard[:, t:t + 1], None, ALU.subtract)\
                        .then_inc(guarded, 1)

            def guard_heads(o):
                si = wh[:, :, D:D + H]
                sj = wh[:, :, D + H:D + 2 * H]
                m = mall[:, :].unsqueeze(1).broadcast_to([P, T, H])
                dve.wait_ge(read["wh"], o.count(2, 2))
                dve.tensor_reduce(mloc[:, :], si.rearrange("p t h -> p h t"), AX_X, ALU.max).then_inc(mloc_made, 1)
                dve.tensor_scalar(steepsi[:, :, :], si, STEEP, None, ALU.mult)
                dve.wait_ge(mall_made, o.count(1, 1))
                dve.tensor_tensor(exin[:, 0, :, :], si, m, ALU.subtract).then_inc(exin_made, 1)
                dve.tensor_tensor(wsj[:, :, :], sj, m, ALU.add).then_inc(exin_made, 1)
                dve.wait_ge(exin_made, o.count(5, 1))
                dve.tensor_scalar(exin[:, 1, :, :], exin[:, 0, :, :], SLOPE2, None, ALU.mult).then_inc(exin_made, 1)
                dve.wait_ge(exin_made, o.count(5, 2))
                dve.tensor_scalar(exin[:, 2, :, :], wsj[:, :, :], 0.0, 1.0 - SLOPE2, ALU.min, ALU.mult)\
                    .then_inc(exin_made, 1)
                dve.tensor_scalar(exin[:, 3, :, :], wsj[:, :, :], 0.0, SLOPE2 - 1.0, ALU.max, ALU.mult)\
                    .then_inc(exin_made, 1)

            def split_values(o):
                v = vals[:, :, :, :].rearrange("p t h c -> p (t h) c")
                part = [vparts[:, :, :, n, :].rearrange("p t h c -> p (t h) c") for n in range(3)]
                dve.wait_ge(vals_made, o.count(4, 4))
                dve.tensor_copy(part[0], v).then_inc(vsplit, 1)
                dve.wait_ge(vsplit, o.count(4, 1))
                dve.tensor_tensor(v, v, part[0], ALU.subtract).then_inc(vsplit, 1)
                dve.wait_ge(vsplit, o.count(4, 2))
                dve.tensor_copy(part[1], v).then_inc(vsplit, 1)
                dve.wait_ge(vsplit, o.count(4, 3))
                dve.tensor_tensor(part[2], v, part[1], ALU.subtract).then_inc(vsplit, 1)

            def mins(o, h):
                if h == 1:
                    dve.wait_ge(vsplit, o.count(4, 4))
                elif h == 2 and (o.turn is not None or o.base < NB - 1):
                    dve.wait_ge(full["st"], o.count(T, 2 * T))
                elif h == 3:
                    dve.wait_ge(full["c"], o.count(2 * H, 2))
                for t in range(T):
                    n = h * T + t
                    dve.wait_ge(step_made, o.count(H * T, n + 1))
                    dve.tensor_tensor(C_OF[h][:, t, :], steps[:, n % 2, :], adjs[o.parity][:, t, :], ALU.min)\
                        .then_inc(c_made, 1)

            def context(g, k):
                zq = quarters(Z)
                dve.wait_ge(probs_used, g.count(T, 4 * k + 4))
                dve.reciprocal(rden[:, 4 * k:4 * k + 4], zq[:, :, D]).then_inc(rden_made, 1)
                dve.wait_ge(rden_made, g.count(2, k + 1))
                if k == 0:
                    dve.wait_ge(x0_biased, g.count(1, 1))
                for j in range(4):
                    t = 4 * k + j
                    ins = dve.scalar_tensor_tensor(x1[:, t, :], zq[:, j, 0:D], rden[:, t:t + 1], x0[:, t, :],
                                                   ALU.mult, ALU.add)
                ins.then_inc(y_made[0], 1)

            def norm_stats(layer, g, xn, k):
                dve.wait_ge(y_made[layer], g.count(2, k + 1))
                for t in range(4 * k, 4 * k + 4):
                    ins = dve.bn_stats(stats[:, t, :], xn[:, t, :])
                ins.then_inc(stats_made[layer], 1)
                dve.wait_ge(stats_made[layer], g.count(2, k + 1))
                dve.nop(nofuse=True)
                for t in range(4 * k, 4 * k + 4):
                    ins = dve.bn_aggr(meanvar[:, layer, t, :], stats[:, t, :])
                ins.then_inc(meanvar_made[layer], 1)

            def norm_apply(layer, g, xn, k):
                dve.wait_ge(rstd_made[layer], g.count(2, k + 1))
                for t in range(4 * k, 4 * k + 4):
                    ins = dve.tensor_scalar(xn[:, t, :], xn[:, t, :], meanvar[:, layer, t, 0:1], rstd[:, layer, t:t + 1],
                                            ALU.subtract, ALU.mult)
                ins.then_inc(normed[layer], 1)

            def split_half(parts, k, src, done, g, per, at):
                left = rest[:, :].rearrange("p (t d) -> p t d", d=D)
                ts = slice(4 * k, 4 * k + 4)
                dve.tensor_copy(parts[:, 0, ts, :], src).then_inc(done, 1)
                dve.wait_ge(done, g.count(per, at + 1))
                dve.tensor_tensor(left, src, parts[:, 0, ts, :], ALU.subtract).then_inc(done, 1)
                dve.wait_ge(done, g.count(per, at + 2))
                dve.tensor_copy(parts[:, 1, ts, :], left).then_inc(done, 1)
                dve.wait_ge(done, g.count(per, at + 3))
                dve.tensor_tensor(parts[:, 2, ts, :], left, parts[:, 1, ts, :], ALU.subtract).then_inc(done, 1)

            def split_x1(g, k):
                dve.wait_ge(normed[0], g.count(2, k + 1))
                split_half(parts1, k, x1[:, 4 * k:4 * k + 4, :], split1, g, 8, 4 * k)

            def split_x3(o, k):
                left = rest[:, :].rearrange("p (t d) -> p t d", d=D)
                dve.wait_ge(normed[2], o.count(2, k + 1))
                for j in range(4):
                    t = 4 * k + j
                    ins = dve.tensor_scalar(left[:, j, :], x3[:, t, :], dcol[o.parity][:, t:t + 1], None, ALU.mult)
                ins.then_inc(split3, 1)
                dve.wait_ge(split3, o.count(10, 5 * k + 1))
                split_half(parts3, k, left, split3, o, 10, 5 * k + 1)

            def sums_of_masks(kind, o):
                for k in range(2):
                    dve.wait_ge(full["mask"], o.count(2, k + 1))
                    dve.tensor_copy(msum[:, 4 * k:4 * k + 4, :], quarters(slot(kind, "mask", k))[:, :, 0:H * HW])\
                        .then_inc(read["mask"], 1)

            def sums_of_head(kind, o, h):
                for k in range(2):
                    n = 2 * h + k
                    if h >= 2 and k == 0:
                        dve.wait_ge(num_made, o.count(4 * H, 4 * (h - 1)))
                    dve.wait_ge(full["c"], o.count(2 * H, n + 1))
                    src = quarters(slot(kind, "c", n))[:, :, 0:3 * VW].rearrange("p t (s c) -> p t c s", s=3)
                    dve.tensor_reduce(csum[:, h % 2, 4 * k:4 * k + 4, :], src, AX_X, ALU.add).then_inc(read["c"], 1)

            def head_out(o, h):
                cols = slice(h * DH, (h + 1) * DH)
                dve.wait_ge(num_made, o.count(4 * H, 4 * h + 4))
                dve.reciprocal(rgat[:, :], num[:, :, DH]).then_inc(rgat_made, 1)
                dve.wait_ge(rgat_made, o.count(H, h + 1))
                dve.tensor_tensor(gatout[:, :, :], num[:, :, 0:DH], rgat[:, :].unsqueeze(2).broadcast_to([P, T, DH]),
                                  ALU.mult).then_inc(gat_made, 1)
                dve.wait_ge(gat_made, o.count(H, h + 1))
                if h == 0 and (o.turn is not None or o.base > 0):
                    dve.wait_ge(stored, o.count(16))
                for k in range(2):
                    ts = slice(4 * k, 4 * k + 4)
                    ins = dve.tensor_tensor(x3[:, ts, cols], gatout[:, ts, :], x2[:, ts, cols], ALU.add)
                    if h == H - 1:
                        ins.then_inc(y_made[2], 1)

            def layer1_out(kind, g, k):
                s = by_tile(slot(kind, "out1", k))
                half = x2[:, 4 * k:4 * k + 4, :]
                dve.wait_ge(full["out1"], g.count(2, k + 1))
                if k == 0:
                    dve.wait_ge(degrees, g.count(3, 3))
                for j in range(4):
                    t = 4 * k + j
                    ins = dve.scalar_tensor_tensor(x2[:, t, :], s[:, j, :], rrow[:, t:t + 1], b1_s[:, :], ALU.mult, ALU.add)
                ins.then_inc(read["out1"], 1)
                dve.wait_ge(read["out1"], g.count(2, k + 1))
                dve.scalar_tensor_tensor(half, half, SLOPE1, half, ALU.mult, ALU.max).then_inc(z1_made, 1)
                dve.wait_ge(z1_made, g.count(2, k + 1))
                dve.tensor_tensor(half, half, x1[:, 4 * k:4 * k + 4, :], ALU.add).then_inc(y_made[1], 1)

            def layer3_out(kind, o, k):
                s = by_tile(slot(kind, "out3", k))
                dve.wait_ge(full["out3"], o.count(2, k + 1))
                for j in range(4):
                    t = 4 * k + j
                    ins = dve.scalar_tensor_tensor(x3[:, t, :], s[:, j, :], dcol[o.parity][:, t:t + 1], x3[:, t, :],
                                                   ALU.mult, ALU.add)
                ins.then_inc(y_made[3], 1)

            make_maskb(Graph(0))

            def step(kind, g):
                o = g.before()
                if kind != "last":
                    guards(kind, g)
                if kind != "first":
                    guard_heads(o)
                    mins(o, 0)
                if kind != "last":
                    context(g, 0)
                    norm_stats(0, g, x1, 0)
                if kind != "first":
                    split_values(o)
                if kind != "last":
                    norm_apply(0, g, x1, 0)
                    split_x1(g, 0)
                if kind != "first":
                    mins(o, 1)
                if kind != "last":
                    context(g, 1)
                    norm_stats(0, g, x1, 1)
                if kind != "first":
                    mins(o, 2)
                if kind != "last":
                    norm_apply(0, g, x1, 1)
                    split_x1(g, 1)
                if kind != "first":
                    sums_of_masks(kind, o)
                    sums_of_head(kind, o, 0)
                    mins(o, 3)
                    head_out(o, 0)
                    for h in range(1, H):
                        sums_of_head(kind, o, h)
                        head_out(o, h)
                    norm_stats(2, o, x3, 0)
                    norm_stats(2, o, x3, 1)
                    for k in range(2):
                        norm_apply(2, o, x3, k)
                        split_x3(o, k)
                if kind != "last":
                    for k in range(2):
                        layer1_out(kind, g, k)
                        norm_stats(1, g, x2, k)
                    norm_apply(1, g, x2, 0)
                    norm_apply(1, g, x2, 1)
                    if g.turn is not None or g.base < NB - 1:
                        make_maskb(Graph(g.base + 1, g.turn))
                if kind != "first":
                    for k in range(2):
                        layer3_out(kind, o, k)
                        norm_stats(3, o, x3, k)
                    norm_apply(3, o, x3, 0)
                    norm_apply(3, o, x3, 1)

            program(dve, step)

        @block.tensor
        def _(pe):
            pe.wait_ge(ident_made, 2)
            pe.wait_ge(dve_init, 5)
            pe.wait_ge(pool_init, 3)
            pe.wait_ge(consts_in, 16 * 10)
            pe.matmul(ring[0][:, 0, 0:D], wq_s[:, :], wk_s[:, :], start=True, stop=True)
            pe.matmul(ring[0][:, 1, 0:1], wk_s[:, :], bqcol[:, 0:1], start=True, stop=True).then_inc(wqk_full, 1)
            pe.wait_ge(act_init, 1)

            def claim(kind, g, name, k):
                n = ORDER[kind].index((name, k))
                if n >= SLOTS:
                    (was, j), of = ORDER[kind][n - SLOTS], g
                elif kind == "first":
                    return slot(kind, name, k)
                elif g.turn is None and g.base == 1:
                    (was, j), of = ORDER["first"][n - SLOTS], g.before()
                else:
                    (was, j), of = ORDER["full"][n - SLOTS], g.before()
                if was in OLDER:
                    of = of.before()
                if was == "out3":
                    pe.wait_ge(y_made[3], of.count(2, j + 1))
                else:
                    pe.wait_ge(read[was], of.count(PER[was], j + 1))
                return slot(kind, name, k)

            def transposes(kind, g, h, name, src):
                s = whole(claim(kind, h, name, 0))
                for t in range(T):
                    last = pe.transpose(s[:, t * P:(t + 1) * P], src[:, t, :], identf[:, :])
                last.then_inc(full[name], 1)

            def project(kind, g):
                pe.wait_ge(x_in, g.count(16, 16))
                transposes(kind, g, g, "xT", x0)
                pe.wait_ge(read["xT"], g.count(1, 1))
                s = claim(kind, g, "q", 0)
                for c in range(2):
                    last = pe.matmul(s[:, c, :], wqk[:, :], xT[:, c * 512:(c + 1) * 512], start=True, stop=True)
                last.then_inc(full["q"], 1)
                s = by_tile(claim(kind, g, "v", 0))
                for t in range(T):
                    last = pe.matmul(s[:, t, :], xT[:, t * P:(t + 1) * P], wv_s[:, :], start=True, stop=True)
                last.then_inc(full["v"], 1)

            def transpose_adj(kind, g, m):
                s = by_tile(claim(kind, g, "at", m))
                if m == 0:
                    pe.wait_ge(adj_in[g.parity], g.count_own(16, 16))
                for t in range(T):
                    last = pe.matmul(s[:, t, :], adjs[g.parity][:, t, m * P:(m + 1) * P], ident16[:, :],
                                     start=True, stop=True)
                last.then_inc(full["at"], 1)

            def guard_scores(kind, g, t):
                s = claim(kind, g, "s", t)
                if t == 0:
                    pe.wait_ge(read["q"], g.count(1, 1))
                for c in range(2):
                    last = pe.matmul(s[:, c, :], qb[:, t * P:(t + 1) * P], xb[:, c * 512:(c + 1) * 512],
                                     start=True, stop=True)
                last.then_inc(full["s"], 1)

            def head_inputs(kind, g, name, k):
                o = g.before()
                if name == "x2T":
                    pe.wait_ge(normed[1], o.count(2, 2))
                    transposes(kind, o, g, "x2T", x2)
                elif name == "wh":
                    s = quarters(claim(kind, g, "wh", k))
                    if k == 0:
                        pe.wait_ge(read["x2T"], o.count(1, 1))
                    for j in range(4):
                        t = 4 * k + j
                        last = pe.matmul(s[:, j, 0:D + 2 * H], x2T[:, t * P:(t + 1) * P], wext[:, :], start=True, stop=True)
                    last.then_inc(full["wh"], 1)
                else:
                    s = claim(kind, g, "sj", 0)
                    for c in range(2):
                        last = pe.matmul(s[0:H, c, :], wext[:, D + H:D + 2 * H], x2T[:, c * 512:(c + 1) * 512],
                                         start=True, stop=True)
                    last.then_inc(full["sj"], 1)

            def scores(kind, g, n):
                c = n // 4
                s = claim(kind, g, "st", n)
                for j in range(2):
                    kt = 2 * (n % 4) + j
                    if n % 4 == 0 and j == 0:
                        pe.wait_ge(guarded, g.count(T, 4 * c + 4))
                    for q in range(4):
                        pe.matmul(s[:, j, q * P:(q + 1) * P], maskb[:, 4 * c + q, kt * P:(kt + 1) * P],
                                  ident16[:, :], start=q == 0, stop=False, skip_group_check=True)
                    last = pe.matmul(s[:, j, :], xT[:, kt * P:(kt + 1) * P], qT[:, c * 512:(c + 1) * 512],
                                     start=False, stop=True, skip_group_check=True)
                last.then_inc(full["st"], 1)

            def context(g, n):
                c = n // 4
                zq = quarters(Z)
                if n == 0:
                    pe.wait_ge(read["v"], g.count(1, 1))
                    if g.turn is not None or g.base > 1:
                        pe.wait_ge(read["agg3"], g.before(2).count(1, 1))
                    if g.turn is not None or g.base > 0:
                        pe.wait_ge(read["agg1"], g.count(1))
                elif n == 4:
                    pe.wait_ge(y_made[0], g.count(2, 1))
                pe.wait_ge(read["st"], g.count(T, n + 1))
                for j in range(2):
                    kt = 2 * (n % 4) + j
                    for q in range(4):
                        last = pe.matmul(zq[:, q, 0:D + 1], probs[:, n % 2, j, q * P:(q + 1) * P], vv[:, kt, :],
                                         start=kt == 0 and q % 2 == 0, stop=kt == T - 1, skip_group_check=True)
                last.then_inc(probs_used, 1)

            def mask_sums(kind, g, k):
                o = g.before()
                s = quarters(claim(kind, g, "mask", k))
                if k == 0:
                    pe.wait_ge(vsplit, o.count(4, 4))
                for j in range(4):
                    jt = 4 * k + j
                    for t in range(T):
                        for part in range(3):
                            last = pe.matmul(s[:, j, 0:H * HW], adjs[o.parity][:, t, jt * P:(jt + 1) * P],
                                             vparts[:, t, :, part, HW:VW], start=t == 0 and part == 0,
                                             stop=t == T - 1 and part == 2)
                last.then_inc(full["mask"], 1)

            def head_sums(kind, g, n):
                o = g.before()
                h = n // 2
                s = quarters(claim(kind, g, "c", n))
                for j in range(4):
                    jt = 4 * (n % 2) + j
                    for t in range(T):
                        if n % 2 == 0 and j == 0:
                            pe.wait_ge(c_made, o.count(H * T, h * T + t + 1))
                        last = pe.matmul(s[:, j, 0:3 * VW], C_OF[h][:, t, jt * P:(jt + 1) * P],
                                         vparts[:, t, h, :, :], start=t == 0, stop=t == T - 1)
                last.then_inc(full["c"], 1)

            def aggregate(name, g, parts, mat):
                for t in range(T):
                    for part in range(3):
                        for c in range(2):
                            last = pe.matmul(Z[:, c, :], parts[:, part, t, :], mat[:, t, c * 512:(c + 1) * 512],
                                             start=t == 0 and part == 0, stop=t == T - 1 and part == 2)
                last.then_inc(full[name], 1)

            def layer1(kind, g):
                pe.wait_ge(split1, g.count(8, 8))
                pe.wait_ge(y_made[0], g.count(2, 2))
                pe.wait_ge(read["at"], g.count(T, T))
                aggregate("agg1", g, parts1, adjTs[g.parity])
                pe.wait_ge(read["agg1"], g.count(1, 1))
                for k in range(2):
                    s = by_tile(claim(kind, g, "out1", k))
                    for j in range(4):
                        t = 4 * k + j
                        last = pe.matmul(s[:, j, :], agg1T[:, t * P:(t + 1) * P], w1_s[:, :], start=True, stop=True)
                    last.then_inc(full["out1"], 1)

            def layer3(kind, g):
                o = g.before()
                pe.wait_ge(split3, o.count(10, 10))
                pe.wait_ge(diag_added, o.count(1, 1))
                if kind == "last":
                    pe.wait_ge(read["agg1"], o.count(1, 1))
                aggregate("agg3", o, parts3, adjTs[o.parity])
                pe.wait_ge(read["agg3"], o.count(1, 1))
                for k in range(2):
                    s = by_tile(claim(kind, g, "out3", k))
                    for j in range(4):
                        t = 4 * k + j
                        last = pe.matmul(s[:, j, :], agg3T[:, t * P:(t + 1) * P], b3_s[:, :], start=True, stop=True)
                    last.then_inc(full["out3"], 1)

            def step(kind, g):
                if kind != "last":
                    project(kind, g)
                for name, k in {"first": at + s_groups, "full": mixed, "last": heads_up}[kind]:
                    if name == "at":
                        transpose_adj(kind, g, k)
                    elif name == "s":
                        guard_scores(kind, g, k)
                    else:
                        head_inputs(kind, g, name, k)
                if kind != "last":
                    scores(kind, g, 0)
                    for n in range(1, T):
                        scores(kind, g, n)
                        context(g, n - 1)
                    context(g, T - 1)
                if kind != "first":
                    mask_sums(kind, g, 0)
                    mask_sums(kind, g, 1)
                    for n in range(2 * H):
                        head_sums(kind, g, n)
                if kind != "last":
                    layer1(kind, g)
                if kind != "first":
                    layer3(kind, g)

            program(pe, step)


_INS = ['x', 'adj', 'Wq', 'bq', 'Wk', 'WvT', 'bv', 'W1T', 'b1', 'W2', 'a2', 'B3']


def kernel(**inputs):
    import numpy as _np
    import concourse.bacc as _bacc
    from concourse import mybir as _mybir
    from concourse.bass_utils import run_bass_kernel_spmd as _run

    given = {
        'x': inputs['x'], 'adj': inputs['adj'],
        'Wq': inputs['L0_gnn_Wq'], 'bq': inputs['L0_gnn_bq'],
        'Wk': inputs['L0_gnn_Wk'], 'WvT': _np.asarray(inputs['L0_gnn_Wv']).T,
        'bv': inputs['L0_gnn_bv'],
        'W1T': _np.asarray(inputs['L1_gnn_W']).T, 'b1': inputs['L1_gnn_b'],
        'W2': inputs['L2_gnn_W'], 'a2': inputs['L2_gnn_a'], 'B3': inputs['L3_gnn_B'],
    }
    nc = _bacc.Bacc("TRN2", target_bir_lowering=False, num_devices=1)
    arrays, args = {}, []
    for name in _INS:
        a = _np.ascontiguousarray(given[name])
        arrays[f"in_{name}_dram"] = a
        args.append(nc.dram_tensor(f"in_{name}_dram", a.shape, _mybir.dt.from_np(a.dtype), kind="ExternalInput").ap())
    shape = tuple(inputs['x'].shape)
    args.append(nc.dram_tensor("out_0_dram", shape, _mybir.dt.float32, kind="ExternalOutput").ap())
    gnn_kernel(nc, *args)
    r = _run(nc, [arrays], core_ids=[0])
    return r.results[0]["out_0_dram"]
```

```python
from contextlib import ExitStack

import concourse.bass as bass
from concourse import mybir

F32 = mybir.dt.float32
F16 = mybir.dt.float16
BF16 = mybir.dt.bfloat16
ALU = mybir.AluOpType
ACT = mybir.ActivationFunctionType
AX_X = mybir.AxisListType.X
RMAX = bass.bass_isa.ReduceOp.max

P = 128
EPS = 1e-5
NEG = 10000.0
STEEP = 1e20
SLOPE1 = 0.01
SLOPE2 = 0.2
STEPS = 4
LOWEST = -3.0e38
TO_EIGHTS = 1.5 * 2.0 ** 26


class Graph:

    def __init__(self, base, turn=None):
        self.base, self.turn = base, turn
        self.parity = base % 2

    def before(self, n=1):
        return Graph(self.base - n, self.turn)

    def count(self, per, k=0):
        n = self.base * per + k
        return n if self.turn is None else self.turn * (2 * per) + n

    def count_own(self, per, k):
        n = (self.base // 2) * per + k
        return n if self.turn is None else self.turn * per + n


def gnn_kernel(nc, x, adj, Wq, bq, Wk, WvT, bv, W1T, b1, W2, a2, B3, out):
    NB, N, D = x.shape
    T = N // P
    H = a2.shape[0]
    DH = D // H
    SCALE = float(D) ** -0.5
    VW = 2 * DH + 2
    HW = DH + 1
    assert D == P and T == 8 and NB % 2 == 0

    x_v = x.rearrange("b (t p) d -> b p t d", p=P)
    adj_v = adj.rearrange("b (t p) m -> b p t m", p=P)
    out_v = out.rearrange("b (t p) d -> b p t d", p=P)
    sj_dram = nc.dram_tensor("sj_rows", (H, N), F32).ap()

    at, s_groups = [("at", m) for m in range(T)], [("s", t) for t in range(T)]
    heads_up = [("x2T", 0), ("wh", 0), ("wh", 1), ("sj", 0)]
    opening = [("xT", 0), at[0], at[1], ("q", 0), at[2], ("v", 0), s_groups[0], heads_up[0], s_groups[1], at[3],
               s_groups[2], heads_up[1], s_groups[3], heads_up[2], heads_up[3], s_groups[4]]
    first_opening = [("xT", 0), ("q", 0), ("v", 0)] + s_groups[:4] + at[:3] + [s_groups[4]]
    soft = [("st", g) for g in range(T)]
    between_scores = s_groups[5:] + at[4:] + [None]
    first_between = s_groups[5:] + at[3:]
    softmax = [group for pair in zip(soft, between_scores) for group in pair if group]
    first_softmax = [group for pair in zip(soft, first_between) for group in pair]
    gat = [("mask", 0), ("mask", 1)] + [("c", g) for g in range(2 * H)]
    ORDER = {
        "first": first_opening + first_softmax + [("out1", 0), ("out1", 1)],
        "full": opening + softmax + gat + [("out1", 0), ("out1", 1), ("out3", 0), ("out3", 1)],
        "last": heads_up + gat[2:4] + gat[:2] + gat[4:] + [("out3", 0), ("out3", 1)],
    }
    every_tile = [(h, t) for h in range(H) for t in range(T)]
    STEP_TILES = {"full": every_tile, "last": [(h, t) for h, t in every_tile if t % 4 != 3]}
    ROWS = {"full": [0, 1, 2, 3], "last": [1, 2, 3]}
    assert H == 4
    PIECES = {"full": [slice(0, H // 2), slice(H // 2, H)], "last": [slice(h, h + 1) for h in range(H)]}
    NP = len(PIECES["full"])
    SPLIT_BY_DVE = {"full": 0, "last": 1}
    DIRECT = {"full": H - 1, "last": 1}
    PACE = [0, 2, 2, 3, 3, 2, 2, 3]
    SLOTS = 3
    assert len(ORDER["full"]) % SLOTS == 0
    SHIFT = {"first": -len(ORDER["first"]) % SLOTS, "full": 0, "last": 0}
    OLDER = ("x2T", "wh", "sj", "mask", "c", "out3")

    ctx = ExitStack()
    with ctx:
        def sb(name, shape, dt):
            return ctx.enter_context(nc.sbuf_tensor(name, shape, dt))

        def sem(name):
            return ctx.enter_context(nc.semaphore(name))

        adjs = [sb(f"adj{p}", [P, T, N], F16) for p in range(2)]
        adjTs = [sb(f"adjT{p}", [P, T, N], F16) for p in range(2)]
        maskb = sb("maskb", [P, T, N], F16)
        cmat = sb("cmat", [P, 2, T, N], F16)
        C_OF = [cmat[:, 0, :, :], cmat[:, 1, :, :], maskb[:, :, :], cmat[:, 0, :, :]]
        C_LAST = [cmat[:, 0, :, :], cmat[:, 1, :, :], adjTs[NB % 2][:, :, :], maskb[:, :, :]]

        def values_in(buffer):
            return buffer.rearrange("p t n -> p (t n)")[:, 0:2 * T * H * VW].bitcast(F32)\
                .rearrange("p (t h c) -> p t h c", h=H, c=VW)

        VALS = {"full": values_in(cmat[:, 1, :, :]), "last": values_in(adjs[NB % 2][:, :, :])}
        probs = sb("probs", [P, 2, 2, 512], F32)
        msum = probs[:, :, :, :].rearrange("p a b c -> p (a b c)")[:, 0:T * H * HW]\
            .rearrange("p (t c) -> p t c", t=T)
        x0 = sb("x0", [P, T, D], F32)
        x1 = sb("x1", [P, T, D], F32)
        x2 = sb("x2", [P, T, D], F32)
        x3 = sb("x3", [P, T, D], F32)
        parts1 = sb("parts1", [P, 3, T, D], BF16)
        xT = sb("xT", [P, N], F32)
        qT = sb("qT", [P, N], F32)
        x2T = sb("x2T", [P, N], F32)
        agg1T, agg3T = qT, x2T
        vparts = sb("vparts", [P, T, H, 3, VW], BF16)
        flat = vparts[:, :, :, :, :].rearrange("p t h s c -> p (t h s c)")
        flat1 = parts1[:, :, :, :].rearrange("p s t d -> p (s t d)")
        qb, xb = flat1[:, 0:N], flat1[:, N:2 * N]
        parts3 = flat[:, 0:3 * N].rearrange("p (s t d) -> p s t d", s=3, d=D)
        vv = sb("vv", [P, T, D + 1], F32)
        wh = sb("wh", [P, T, D + 2 * H], F32)
        sjrow = sb("sjrow", [P, 2, N], F32)
        steps = sb("steps", [P, STEPS, N], BF16)
        csum = sb("csum", [P, 2, T, VW], F32)
        abc = csum[:, 0, :, :].rearrange("p t c -> p (t c)")[:, 0:2 * D]\
            .rearrange("p (h s d) -> p h s d", h=H, s=2)
        sjT = csum[0:H, :, :, :].rearrange("p a t c -> p (a t c)")[:, 0:N]
        num = sb("num", [P, T, HW], F32)
        num2 = sb("num2", [P, T, HW], F32)
        gatout = sb("gatout", [P, T, DH], F32)
        rest = sb("rest", [P, 4 * D], F32)

        identf = sb("identf", [P, P], F32)
        ident16 = sb("ident16", [P, P], F16)
        wq_s = sb("wq_s", [P, D], F32)
        wk_s = sb("wk_s", [P, D], F32)
        wqk = sb("wqk", [P, D], F32)
        wv_s = sb("wv_s", [P, D], F32)
        w1_s = sb("w1_s", [P, D], F32)
        b3_s = sb("b3_s", [P, D], F32)
        wext = sb("wext", [P, D + 2 * H], F32)
        bv_s = sb("bv_s", [P, D], F32)
        b1_s = sb("b1_s", [P, D], F32)
        bqcol = sb("bqcol", [P, 2], F32)
        powers = sb("powers", [P, T, 2], F32)

        rowacc = sb("rowacc", [P, T], F32)
        degree = sb("degree", [P, T], F32)
        rrow = sb("rrow", [P, T], F32)
        dcol = [sb(f"dcol{p}", [P, T], F32) for p in range(2)]
        smax = sb("smax", [P, T], F32)
        guard = sb("guard", [P, T], F32)
        rden = sb("rden", [P, T], F32)
        rgat = sb("rgat", [P, T], F32)
        mloc = sb("mloc", [P, H], F32)
        mall = sb("mall", [P, H], F32)
        wsj = sb("wsj", [P, T, H], F32)
        exin = sb("exin", [P, 4, T, H], F32)
        ex = sb("ex", [P, 4, T, H], F32)
        steepsi = sb("steepsi", [P, T, H], F32)
        minussi = sb("minussi", [P, T, H], F32)
        stats = sb("stats", [P, T, 6], F32)
        meanvar = sb("meanvar", [P, 4, T, 2], F32)
        vareps = sb("vareps", [P, 4, T], F32)
        rstd = sb("rstd", [P, 4, T], F32)
        drstd = sb("drstd", [P, T], F32)

        ring = [ctx.enter_context(nc.psum_tensor(f"ring{s}", [P, 2, 512], F32)) for s in range(SLOTS)]
        Z = ctx.enter_context(nc.psum_tensor("Z", [P, 2, 512], F32))

        qk_in = sem("qk_in")
        wv_in = sem("wv_in")
        bv_in = sem("bv_in")
        heads_in = sem("heads_in")
        late_in = sem("late_in")
        x_in = sem("x_in")
        adj_in = [[sem(f"adj_in{p}_half{k}") for k in range(2)] for p in range(2)]
        stored = sem("stored")
        ident_made = sem("ident_made")
        dve_init = sem("dve_init")
        pool_init = sem("pool_init")
        act_init = sem("act_init")
        wqk_full = sem("wqk_full")
        full = {n: sem(f"{n}_full") for n in
                ("xT", "q", "v", "at", "s", "st", "agg1", "out1", "x2T", "wh", "sj", "mask", "c", "agg3", "out3")}
        read = {n: sem(f"{n}_read") for n in full if n != "out3"}
        PER = {"xT": 1, "q": 1, "v": 1, "at": T, "s": T, "st": T, "agg1": 2, "out1": 2,
               "x2T": 1, "wh": 2, "sj": 1, "mask": 2, "c": 2 * H, "agg3": 2, "out3": 2}
        x0_biased = sem("x0_biased")
        xb_made = sem("xb_made")
        qb_made = sem("qb_made")
        maskb_made = sem("maskb_made")
        rowsums = sem("rowsums")
        degrees = sem("degrees")
        guard_made = sem("guard_made")
        guarded = sem("guarded")
        sj_kept = sem("sj_kept")
        sj_in = [sem("sj_in0"), sem("sj_in1")]
        probs_used = sem("probs_used")
        rden_made = sem("rden_made")
        y_made = [sem(f"y_made{n}") for n in range(4)]
        stats_made = [sem(f"stats_made{n}") for n in range(4)]
        meanvar_made = [sem(f"meanvar_made{n}") for n in range(4)]
        vareps_made = [sem(f"vareps_made{n}") for n in range(4)]
        rstd_made = [sem(f"rstd_made{n}") for n in range(4)]
        drstd_made = sem("drstd_made")
        centred = sem("centred")
        normed = [sem(f"normed{n}") for n in range(4)]
        split1 = sem("split1")
        split3 = sem("split3")
        z1_made = sem("z1_made")
        mloc_made = sem("mloc_made")
        minussi_made = sem("minussi_made")
        mall_made = sem("mall_made")
        exin_made = sem("exin_made")
        ex_made = sem("ex_made")
        vals_made = sem("vals_made")
        high_made = sem("high_made")
        rest_made = sem("rest_made")
        middle_made = sem("middle_made")
        low_made = sem("low_made")
        first_split = sem("first_split")
        sjb_full = sem("sjb_full")
        sjb_read = sem("sjb_read")
        step_made = sem("step_made")
        c_made = sem("c_made")
        num_made = sem("num_made")
        direct_num = sem("direct_num")
        rgat_made = sem("rgat_made")
        gat_made = sem("gat_made")
        diag_added = sem("diag_added")

        block = ctx.enter_context(nc.Block())

        def slot(kind, name, k):
            return ring[(ORDER[kind].index((name, k)) + SHIFT[kind]) % SLOTS]

        def quarters(slot_):
            return slot_[:, :, :].rearrange("p b (a c) -> p (b a) c", a=2)

        def whole(slot_):
            return slot_[:, :, :].rearrange("p b c -> p (b c)")

        def by_tile(slot_):
            return whole(slot_).rearrange("p (t c) -> p t c", c=P)

        def rows_in(kind, o, h):
            return o.count(32, 16 * sum(1 for row in ROWS[kind] if row % 2 == h % 2 and row <= h))

        def program(engine, step):
            step("first", Graph(0))
            step("full", Graph(1))
            with engine.Fori(0, NB // 2 - 2) as turn:
                step("full", Graph(2, turn))
                step("full", Graph(3, turn))
            step("full", Graph(NB - 2))
            step("full", Graph(NB - 1))
            step("last", Graph(NB))

        @block.sync
        def _(sp):
            def load(dst, src, loaded):
                sp.dma_start(dst, src).then_inc(loaded, 16)

            def on_all_partitions(row, n):
                return row.rearrange("(a d) -> a d", a=1).broadcast_to([P, n])

            load(wq_s[:, :], Wq, qk_in)
            load(wk_s[:, :], Wk, qk_in)
            load(bqcol[:, 0:1], bq.rearrange("(p a) -> p a", a=1), qk_in)
            load(wv_s[:, :], WvT, wv_in)
            load(bv_s[:, :], on_all_partitions(bv, D), bv_in)
            load(wext[:, 0:D], W2, heads_in)
            load(csum[:, 0, :, :].rearrange("p t c -> p (t c)")[:, 0:2 * D],
                 a2.rearrange("(a h) c -> a (h c)", a=1).broadcast_to([P, 2 * D]), heads_in)
            load(w1_s[:, :], W1T, late_in)
            load(b1_s[:, :], on_all_partitions(b1, D), late_in)
            load(b3_s[:, :], B3, late_in)

            def number(g):
                return g.base if g.turn is None else g.turn * 2 + g.base

            def spread_sj(o):
                sp.wait_ge(read["sj"], o.count(1, 1))
                sp.dma_start(sj_dram, sjT).then_inc(sj_kept, 16)
                sp.wait_ge(sj_kept, o.count(16, 16))

            def fetch_sj(kind, o, h):
                if h >= 2:
                    sp.wait_ge(step_made, o.count(H * T, sum(1 for tile in STEP_TILES[kind] if tile[0] < h - 1)))
                    if kind == "last":
                        sp.wait_ge(c_made, o.count(H * T, (h - 1) * T))
                sp.dma_start(sjrow[:, h % 2, :], sj_dram[h:h + 1, :].broadcast_to([P, N])).then_inc(sj_in[h % 2], 16)

            def store(g):
                for k in range(2):
                    ts = slice(4 * k, 4 * k + 4)
                    sp.wait_ge(normed[3], g.count(2, k + 1))
                    sp.dma_start(out_v[number(g)][:, ts, :], x3[:, ts, :]).then_inc(stored, 16)

            def step(kind, g):
                o = g.before()
                if kind != "first":
                    spread_sj(o)
                    for h in ROWS[kind]:
                        if kind == "full" and h == 2 and (g.turn is not None or g.base > 1):
                            store(o.before())
                        fetch_sj(kind, o, h)
                if kind == "last":
                    store(o.before())
                if kind != "last" and (g.turn is not None or g.base < NB - 1):
                    sp.wait_ge(y_made[0], g.count(2, 2))
                    sp.dma_start(x0[:, :, :], x_v[number(Graph(g.base + 1, g.turn))]).then_inc(x_in, 16)

            program(sp, step)
            store(Graph(NB - 1))
            sp.wait_ge(stored, 32 * NB)

        @block.gpsimd
        def _(pool):
            def load_adj(g):
                n = g.base if g.turn is None else g.turn * 2 + g.base
                for k in range(2):
                    ts = slice(4 * k, 4 * k + 4)
                    pool.dma_start(adjs[g.parity][:, ts, :], adj_v[n][:, ts, :]).then_inc(adj_in[g.parity][k], 16)

            pool.memset(identf[:, :], 0.0).then_inc(ident_made, 1)
            pool.wait_ge(ident_made, 1)
            pool.affine_select(out=identf[:, :], in_=identf[:, :], compare_op=ALU.not_equal, fill=1.0,
                               base=0, pattern=[[-1, P]], channel_multiplier=1).then_inc(ident_made, 1)
            load_adj(Graph(0))
            load_adj(Graph(1))
            pool.memset(powers[:, :, 0], -0.5).then_inc(pool_init, 1)
            pool.memset(powers[:, :, 1], -1.0).then_inc(pool_init, 1)
            pool.memset(vv[:, :, D:D + 1], 1.0).then_inc(pool_init, 1)
            pool.wait_ge(pool_init, 3)
            pool.wait_ge(bv_in, 16)

            def bias_x0(g):
                pool.wait_ge(full["xT"], g.count(1, 1))
                pool.tensor_tensor(x0[:, :, :], x0[:, :, :], bv_s[:, :].unsqueeze(1).broadcast_to([P, T, D]),
                                   ALU.add).then_inc(x0_biased, 1)

            def degree_of(g):
                pool.wait_ge(rowsums, g.count(T, T))
                pool.nop(nofuse=True)
                pool.tensor_scalar(degree[:, :], rowacc[:, :], 1.0, None, ALU.add).then_inc(degrees, 1)
                pool.tensor_tensor(rrow[:, :], rowacc[:, :], powers[:, :, 1], ALU.pow).then_inc(degrees, 1)
                pool.wait_ge(degrees, g.count(3, 1))
                pool.tensor_tensor(dcol[g.parity][:, :], degree[:, :], powers[:, :, 0], ALU.pow).then_inc(degrees, 1)

            def rstd_of(layer, g, halves=range(2)):
                for k in halves:
                    ts = slice(4 * k, 4 * k + 4)
                    pool.wait_ge(meanvar_made[layer], g.count(2, k + 1))
                    pool.nop(nofuse=True)
                    pool.tensor_scalar(vareps[:, layer, ts], meanvar[:, layer, ts, 1], EPS, None, ALU.add)\
                        .then_inc(vareps_made[layer], 1)
                    pool.wait_ge(vareps_made[layer], g.count(2, k + 1))
                    pool.tensor_tensor(rstd[:, layer, ts], vareps[:, layer, ts], powers[:, 0:4, 0], ALU.pow)\
                        .then_inc(rstd_made[layer], 1)
                    if layer == 2:
                        pool.wait_ge(rstd_made[2], g.count(2, k + 1))
                        pool.tensor_tensor(drstd[:, ts], rstd[:, 2, ts], dcol[g.parity][:, ts], ALU.mult)\
                            .then_inc(drstd_made, 1)

            def norm_apply(layer, g, xn, k):
                ts = slice(4 * k, 4 * k + 4)
                pool.tensor_tensor(xn[:, ts, :], xn[:, ts, :], meanvar[:, layer, ts, 0:1].broadcast_to([P, 4, D]),
                                   ALU.subtract).then_inc(centred, 1)
                pool.wait_ge(centred, g.count(2, k + 1))
                pool.tensor_tensor(xn[:, ts, :], xn[:, ts, :], rstd[:, layer, ts].unsqueeze(2).broadcast_to([P, 4, D]),
                                   ALU.mult).then_inc(normed[layer], 1)

            def largest_si(o):
                pool.wait_ge(mloc_made, o.count(1, 1))
                pool.nop(nofuse=True)
                pool.partition_all_reduce(mall[:, :], mloc[:, :], P, RMAX).then_inc(mall_made, 1)

            def values_of(kind, o, n):
                vals, hs = VALS[kind], PIECES[kind][n]
                if n == 0:
                    pool.wait_ge(ex_made, o.count(1, 1))
                    pool.nop(nofuse=True)
                    for m in range(2):
                        pool.tensor_copy(vals[:, :, :, m * HW + DH], ex[:, m, :, :]).then_inc(vals_made, 1)
                heads = wh[:, :, 0:D].rearrange("p t (h d) -> p t h d", h=H)
                for m in range(2):
                    at = m * HW
                    pool.tensor_tensor(vals[:, :, hs, at:at + DH], heads[:, :, hs, :],
                                       ex[:, m, :, hs].unsqueeze(3).broadcast_to([P, T, hs.stop - hs.start, DH]),
                                       ALU.mult).then_inc(vals_made, 1)

            def take_off(kind, o, n, minus, into, part_made, made):
                hs = PIECES[kind][n]
                v = VALS[kind][:, :, hs, :]
                pool.wait_ge(part_made, o.count(NP, n + 1 - SPLIT_BY_DVE[kind]))
                pool.tensor_tensor(v if into is None else vparts[:, :, hs, into, :], v, vparts[:, :, hs, minus, :],
                                   ALU.subtract).then_inc(made, 1)

            def split_values(kind, o):
                pieces = len(PIECES[kind])
                for n in range(pieces + 2):
                    if n < pieces:
                        values_of(kind, o, n)
                    if 1 + SPLIT_BY_DVE[kind] <= n < pieces + 1:
                        take_off(kind, o, n - 1, 0, None, high_made, rest_made)
                    if kind == "full" and n == 1 and (o.turn is not None or o.base > 0):
                        rstd_of(3, o.before())
                    if n >= 2 + SPLIT_BY_DVE[kind]:
                        take_off(kind, o, n - 2, 1, 2, middle_made, low_made)

            def combine_heads(kind, o):
                for h in range(DIRECT[kind]):
                    pool.wait_ge(read["c"], o.count(2 * H, 2 * h + 2))
                    if h == 0:
                        pool.wait_ge(read["mask"], o.count(2, 2))
                    else:
                        pool.wait_ge(rgat_made, o.count(H + 1, h))
                        pool.wait_ge(gat_made, o.count(H + 1, h))
                    cs = csum[:, h % 2, :, :]
                    f = [ex[:, 2 + n, :, h].unsqueeze(2).broadcast_to([P, T, HW]) for n in range(2)]
                    pool.tensor_tensor(num[:, :, :], msum[:, :, h * HW:(h + 1) * HW], cs[:, :, HW:VW], ALU.subtract)\
                        .then_inc(num_made, 1)
                    pool.tensor_tensor(num2[:, :, :], cs[:, :, 0:HW], f[0], ALU.mult).then_inc(num_made, 1)
                    pool.wait_ge(num_made, o.count(4 * (H - 1), 4 * h + 1))
                    pool.tensor_tensor(num[:, :, :], num[:, :, :], f[1], ALU.mult).then_inc(num_made, 1)
                    pool.wait_ge(num_made, o.count(4 * (H - 1), 4 * h + 3))
                    pool.tensor_tensor(num[:, :, :], num[:, :, :], num2[:, :, :], ALU.add).then_inc(num_made, 1)

            def add_diagonal(g):
                pool.wait_ge(full["agg1"], g.count(2, 2))
                for t in range(T):
                    d = adjTs[g.parity][:, t, t * P:(t + 1) * P]
                    ins = pool.tensor_tensor(d, d, ident16[:, :], ALU.add)
                ins.then_inc(diag_added, 1)

            def step(kind, g):
                o = g.before()
                if kind != "last":
                    bias_x0(g)
                if kind != "first":
                    largest_si(o)
                    split_values(kind, o)
                    if kind == "last":
                        rstd_of(3, o.before())
                if kind != "last":
                    rstd_of(0, g)
                if kind != "first":
                    add_diagonal(o)
                    combine_heads(kind, o)
                    rstd_of(2, o)
                    if o.turn is not None or o.base < NB - 2:
                        pool.wait_ge(full["c"], o.count(2 * H, 2 * H))
                        load_adj(Graph(o.base + 2, o.turn))
                if kind != "last":
                    degree_of(g)
                if kind != "first":
                    for k in range(2):
                        pool.wait_ge(split3, o.count(10, 5 * k + 1))
                        norm_apply(2, o, x3, k)
                if kind != "last":
                    for k in range(2):
                        rstd_of(1, g, [k])

            program(pool, step)
            rstd_of(3, Graph(NB - 1))

        @block.scalar
        def _(act):
            act.dma_start(x0[:, :, :], x_v[0]).then_inc(x_in, 16)

            def take_query_weights():
                act.wait_ge(wqk_full, 1)
                act.activation(wqk[:, :], Z[:, 0, 0:D], ACT.Copy)
                act.activation(bqcol[:, 1:2], Z[:, 1, 0:1], ACT.Copy, scale=SCALE).then_inc(act_init, 1)
                act.wait_ge(act_init, 1)

            def sum_row(g, t):
                if t == 0 and (g.turn is not None or g.base > 0):
                    act.wait_ge(c_made, g.count(H * T))
                    act.wait_ge(degrees, g.count(3))
                if t >= STEPS:
                    act.wait_ge(rowsums, g.count(T, t - STEPS + 1))
                act.activation(steps[:, t % STEPS, :], adjs[g.parity][:, t, :], ACT.Copy,
                               accum_out=rowacc[:, t:t + 1]).then_inc(rowsums, 1)

            def take(kind, g, name, k, dst, src):
                act.wait_ge(full[name], g.count(PER[name], k + 1))
                return act.activation(dst, src, ACT.Copy)

            def make_maskb(g, tiles):
                for t in tiles:
                    if t % 4 == 0:
                        act.wait_ge(full["st"], g.before().count(T, t + 4))
                    if t == 0 and (g.turn is not None or g.base > 1):
                        act.wait_ge(full["c"], g.before().count(2 * H, -2))
                    if t % 4 == 0:
                        act.wait_ge(adj_in[g.parity][t // 4], g.count_own(16, 16))
                    act.activation(maskb[:, t, :], adjs[g.parity][:, t, :], ACT.Copy, bias=-NEG, scale=NEG)\
                        .then_inc(maskb_made, 1)

            def take_sums(name, g, dst, halves=range(2)):
                for c in halves:
                    act.wait_ge(full[name], g.count(2, c + 1))
                    act.activation(dst[:, c * 512:(c + 1) * 512], Z[:, c, :], ACT.Copy).then_inc(read[name], 1)

            def take_group(kind, g, name, k):
                o = g.before()
                src = slot(kind, name, k)
                if name == "xT":
                    take(kind, g, name, k, xT[:, :], whole(src)).then_inc(read[name], 1)
                elif name == "q":
                    if kind == "first":
                        take_query_weights()
                    act.wait_ge(full["q"], g.count(1, 1))
                    act.activation(qT[:, :], whole(src), ACT.Identity, bias=bqcol[:, 1:2], scale=SCALE).then_inc(read["q"], 1)
                elif name == "v":
                    take(kind, g, name, k, vv[:, :, 0:D], by_tile(src)).then_inc(read[name], 1)
                elif name == "at":
                    take(kind, g, name, k, adjTs[g.parity][:, k, :], whole(src)).then_inc(read[name], 1)
                elif name == "x2T":
                    take(kind, o, name, k, x2T[:, :], whole(src)).then_inc(read[name], 1)
                elif name == "wh":
                    take(kind, o, name, k, wh[:, 4 * k:4 * k + 4, :], quarters(src)[:, :, 0:D + 2 * H])\
                        .then_inc(read[name], 1)
                elif name == "sj":
                    if kind == "last":
                        act.wait_ge(sjb_full, 1)
                        act.activation(sjrow[:, 0, :], whole(Z), ACT.Copy).then_inc(sjb_read, 1)
                        factors(o)
                    take(kind, o, name, k, sjT, whole(src)[0:H, :]).then_inc(read[name], 1)

            def factors(o):
                act.wait_ge(exin_made, o.count(5, 5))
                act.activation(ex[:, :, :, :], exin[:, :, :, :], ACT.Exp).then_inc(ex_made, 1)

            def step_tile(kind, o, n):
                h, t = STEP_TILES[kind][n]
                if n >= STEPS:
                    was_h, was_t = STEP_TILES[kind][n - STEPS]
                    act.wait_ge(c_made, o.count(H * T, was_h * T + was_t + 1))
                if t == 0 and h in ROWS[kind]:
                    act.wait_ge(sj_in[h % 2], rows_in(kind, o, h))
                elif t == 0:
                    act.wait_ge(sjb_read, 1)
                act.activation(steps[:, n % STEPS, :], sjrow[:, h % 2, :], ACT.Relu, bias=steepsi[:, t, h:h + 1],
                               scale=STEEP).then_inc(step_made, 1)

            def exp_tile(kind, g, n):
                act.wait_ge(full["st"], g.count(T, n + 1))
                if g.turn is not None or g.base > 0 or n >= 2:
                    act.wait_ge(probs_used, g.count(T, n - 1))
                act.activation(probs[:, n % 2, :, :], slot(kind, "st", n)[:, :, :], ACT.Exp).then_inc(read["st"], 1)

            def step(kind, g):
                o = g.before()
                for name, k in {"first": first_opening, "full": opening, "last": heads_up}[kind]:
                    take_group(kind, g, name, k)
                made = 0
                if kind != "last":
                    for n in range(T):
                        exp_tile(kind, g, n)
                        if kind == "first":
                            take_group(kind, g, *first_between[n])
                            if n < 4:
                                sum_row(g, 2 * n)
                                sum_row(g, 2 * n + 1)
                            else:
                                make_maskb(Graph(1), [n - 4])
                        elif n < T - 1:
                            take_group(kind, g, *between_scores[n])
                        if kind == "full":
                            if n == 0:
                                factors(o)
                            for n_step in range(made, made + PACE[n]):
                                step_tile(kind, o, n_step)
                            made += PACE[n]
                    if kind == "first":
                        make_maskb(Graph(1), range(4, T))
                if kind != "first":
                    for n in range(made, len(STEP_TILES[kind])):
                        step_tile(kind, o, n)
                if kind == "full":
                    for t in range(T):
                        sum_row(g, t)
                if kind != "last":
                    take_sums("agg1", g, agg1T)
                for c in range(2):
                    if kind == "full" and (g.turn is not None or g.base < NB - 1):
                        make_maskb(Graph(g.base + 1, g.turn), range(4 * c, 4 * c + 4))
                    if kind != "first":
                        take_sums("agg3", o, agg3T, [c])

            program(act, step)

        @block.vector
        def _(dve):
            dve.wait_ge(ident_made, 2)
            dve.tensor_copy(ident16[:, :], identf[:, :]).then_inc(dve_init, 1)

            def project_heads():
                dve.wait_ge(heads_in, 32)
                heads = wext[:, 0:D].rearrange("p (h d) -> p h d", h=H)
                for n in range(2):
                    dve.tensor_tensor(rest[:, n * D:(n + 1) * D].rearrange("p (h d) -> p h d", h=H), heads,
                                      abc[:, :, n, :], ALU.mult).then_inc(dve_init, 1)
                for n in range(2):
                    dve.wait_ge(dve_init, 2 + n)
                    dve.tensor_reduce(wext[:, D + n * H:D + (n + 1) * H],
                                      rest[:, n * D:(n + 1) * D].rearrange("p (h d) -> p h d", h=H), AX_X, ALU.add)\
                        .then_inc(dve_init, 1)
                dve.wait_ge(dve_init, 5)

            def make_first_maskb(half):
                dve.wait_ge(adj_in[0][half], 16)
                for t in range(4 * half, 4 * half + 4):
                    dve.tensor_scalar(maskb[:, t, :], adjs[0][:, t, :], NEG, -NEG, ALU.mult, ALU.add)\
                        .then_inc(maskb_made, 1)

            def guards(kind, g, tiles):
                for n in range(tiles.start, tiles.stop + 2):
                    if n < tiles.stop:
                        row_maximum(kind, g, n)
                    if tiles.start < n <= tiles.stop:
                        t = n - 1
                        dve.wait_ge(read["s"], g.count(T, t + 1))
                        dve.tensor_scalar(guard[:, t:t + 1], smax[:, t:t + 1], TO_EIGHTS, -TO_EIGHTS, ALU.add, ALU.add)\
                            .then_inc(guard_made, 1)
                    if n >= tiles.start + 2:
                        t = n - 2
                        dve.wait_ge(guard_made, g.count(T, t + 1))
                        dve.tensor_scalar(maskb[:, t, :], maskb[:, t, :], guard[:, t:t + 1], None, ALU.subtract)\
                            .then_inc(guarded, 1)

            def row_maximum(kind, g, t):
                s = whole(slot(kind, "s", t))
                dve.wait_ge(full["s"], g.count(T, t + 1))
                dve.wait_ge(maskb_made, g.count(T, t + 1))
                dve.nop(nofuse=True)
                dve.tensor_tensor_reduce(out=s, in0=s, in1=maskb[:, t, :], scale=1.0, scalar=LOWEST,
                                         op0=ALU.add, op1=ALU.max, accum_out=smax[:, t:t + 1]).then_inc(read["s"], 1)

            def guard_heads(o):
                si = wh[:, :, D:D + H]
                sj = wh[:, :, D + H:D + 2 * H]
                m = mall[:, :].unsqueeze(1).broadcast_to([P, T, H])
                dve.wait_ge(read["wh"], o.count(2, 2))
                dve.tensor_reduce(mloc[:, :], si.rearrange("p t h -> p h t"), AX_X, ALU.max).then_inc(mloc_made, 1)
                dve.tensor_scalar(steepsi[:, :, :], si, STEEP, None, ALU.mult)
                dve.tensor_scalar(minussi[:, :, :], si, -1.0, None, ALU.mult).then_inc(minussi_made, 1)
                dve.wait_ge(mall_made, o.count(1, 1))
                dve.tensor_tensor(exin[:, 0, :, :], si, m, ALU.subtract).then_inc(exin_made, 1)
                dve.tensor_tensor(wsj[:, :, :], sj, m, ALU.add).then_inc(exin_made, 1)
                dve.wait_ge(exin_made, o.count(5, 1))
                dve.tensor_scalar(exin[:, 1, :, :], exin[:, 0, :, :], SLOPE2, None, ALU.mult).then_inc(exin_made, 1)
                dve.wait_ge(exin_made, o.count(5, 2))
                dve.tensor_scalar(exin[:, 2, :, :], wsj[:, :, :], 0.0, 1.0 - SLOPE2, ALU.min, ALU.mult)\
                    .then_inc(exin_made, 1)
                dve.tensor_scalar(exin[:, 3, :, :], wsj[:, :, :], 0.0, SLOPE2 - 1.0, ALU.max, ALU.mult)\
                    .then_inc(exin_made, 1)

            def take_part(kind, o, n, part):
                hs = PIECES[kind][n]
                if part == 0:
                    dve.wait_ge(vals_made, o.count(2 + 2 * NP, 2 * n + 4))
                else:
                    dve.wait_ge(rest_made, o.count(NP, n + 1 - SPLIT_BY_DVE[kind]))
                dve.tensor_copy(vparts[:, :, hs, part, :], VALS[kind][:, :, hs, :])\
                    .then_inc((high_made, middle_made)[part], 1)

            def mins(kind, o, h, tiles=range(T)):
                c_of = (C_OF if kind == "full" else C_LAST)[h]
                if kind == "full":
                    if h == 1:
                        dve.wait_ge(low_made, o.count(NP, NP))
                    elif h == 2 and (o.turn is not None or o.base < NB - 1):
                        dve.wait_ge(full["st"], o.count(T, 2 * T))
                    elif h == 3:
                        dve.wait_ge(full["c"], o.count(2 * H, 2))
                for t in tiles:
                    if (h, t) in STEP_TILES[kind]:
                        n = STEP_TILES[kind].index((h, t))
                        dve.wait_ge(step_made, o.count(H * T, n + 1))
                        dve.tensor_tensor(c_of[:, t, :], steps[:, n % STEPS, :], adjs[o.parity][:, t, :], ALU.min)\
                            .then_inc(c_made, 1)
                    else:
                        if h in ROWS[kind]:
                            dve.wait_ge(sj_in[h % 2], rows_in(kind, o, h))
                        else:
                            dve.wait_ge(sjb_read, 1)
                            dve.wait_ge(minussi_made, o.count(1, 1))
                        dve.scalar_tensor_tensor(c_of[:, t, :], sjrow[:, h % 2, :], minussi[:, t, h:h + 1],
                                                 adjs[o.parity][:, t, :], ALU.is_ge, ALU.mult).then_inc(c_made, 1)

            def context(g, k):
                zq = quarters(Z)
                dve.wait_ge(probs_used, g.count(T, 4 * k + 4))
                dve.reciprocal(rden[:, 4 * k:4 * k + 4], zq[:, :, D]).then_inc(rden_made, 1)
                dve.wait_ge(rden_made, g.count(2, k + 1))
                if k == 0:
                    dve.wait_ge(x0_biased, g.count(1, 1))
                for j in range(4):
                    t = 4 * k + j
                    ins = dve.scalar_tensor_tensor(x1[:, t, :], zq[:, j, 0:D], rden[:, t:t + 1], x0[:, t, :],
                                                   ALU.mult, ALU.add)
                ins.then_inc(y_made[0], 1)

            def norm_stats(layer, g, xn, k):
                dve.wait_ge(y_made[layer], g.count(2, k + 1))
                for t in range(4 * k, 4 * k + 4):
                    ins = dve.bn_stats(stats[:, t, :], xn[:, t, :])
                ins.then_inc(stats_made[layer], 1)
                dve.wait_ge(stats_made[layer], g.count(2, k + 1))
                dve.nop(nofuse=True)
                for t in range(4 * k, 4 * k + 4):
                    ins = dve.bn_aggr(meanvar[:, layer, t, :], stats[:, t, :])
                ins.then_inc(meanvar_made[layer], 1)

            def norm_apply(layer, g, xn, k):
                dve.wait_ge(rstd_made[layer], g.count(2, k + 1))
                for t in range(4 * k, 4 * k + 4):
                    ins = dve.tensor_scalar(xn[:, t, :], xn[:, t, :], meanvar[:, layer, t, 0:1], rstd[:, layer, t:t + 1],
                                            ALU.subtract, ALU.mult)
                ins.then_inc(normed[layer], 1)

            def split_half(parts, k, src, done, g, per, at):
                left = rest[:, :].rearrange("p (t d) -> p t d", d=D)
                ts = slice(4 * k, 4 * k + 4)
                dve.tensor_copy(parts[:, 0, ts, :], src).then_inc(done, 1)
                dve.wait_ge(done, g.count(per, at + 1))
                dve.tensor_tensor(left, src, parts[:, 0, ts, :], ALU.subtract).then_inc(done, 1)
                dve.wait_ge(done, g.count(per, at + 2))
                dve.tensor_copy(parts[:, 1, ts, :], left).then_inc(done, 1)
                dve.wait_ge(done, g.count(per, at + 3))
                dve.tensor_tensor(parts[:, 2, ts, :], left, parts[:, 1, ts, :], ALU.subtract).then_inc(done, 1)

            def split_x1(g, k):
                dve.wait_ge(normed[0], g.count(2, k + 1))
                split_half(parts1, k, x1[:, 4 * k:4 * k + 4, :], split1, g, 8, 4 * k)

            def split_x3(o, k):
                left = rest[:, :].rearrange("p (t d) -> p t d", d=D)
                dve.wait_ge(drstd_made, o.count(2, k + 1))
                if k == 1:
                    dve.wait_ge(split3, o.count(10, 5))
                for j in range(4):
                    t = 4 * k + j
                    ins = dve.tensor_scalar(left[:, j, :], x3[:, t, :], meanvar[:, 2, t, 0:1], drstd[:, t:t + 1],
                                            ALU.subtract, ALU.mult)
                ins.then_inc(split3, 1)
                dve.wait_ge(split3, o.count(10, 5 * k + 1))
                split_half(parts3, k, left, split3, o, 10, 5 * k + 1)

            def sums_of_masks(kind, o, k):
                dve.wait_ge(full["mask"], o.count(2, k + 1))
                if k == 0 and kind != "last":
                    dve.wait_ge(probs_used, o.count(T, 2 * T))
                dve.tensor_copy(msum[:, 4 * k:4 * k + 4, :], quarters(slot(kind, "mask", k))[:, :, 0:H * HW])\
                    .then_inc(read["mask"], 1)

            def sums_of_head(kind, o, h, k):
                n = 2 * h + k
                if h >= 2 and k == 0:
                    dve.wait_ge(num_made, o.count(4 * (H - 1), 4 * (h - 1)))
                dve.wait_ge(full["c"], o.count(2 * H, n + 1))
                src = quarters(slot(kind, "c", n))[:, :, 0:3 * VW].rearrange("p t (s c) -> p t c s", s=3)
                dve.tensor_reduce(csum[:, h % 2, 4 * k:4 * k + 4, :], src, AX_X, ALU.add).then_inc(read["c"], 1)

            def combine_direct(kind, o, h, k):
                ts, n = slice(4 * k, 4 * k + 4), 6 * (h - DIRECT[kind]) + 3 * k
                sums = quarters(slot(kind, "c", 2 * h + k))
                if k == 0:
                    dve.wait_ge(read["mask"], o.count(2, 2))
                    dve.wait_ge(gat_made, o.count(H + 1, outs(kind, h, 0)))
                dve.wait_ge(full["c"], o.count(2 * H, 2 * h + k + 1))
                f = [ex[:, 2 + n, ts, h].unsqueeze(2).broadcast_to([P, 4, HW]) for n in range(2)]
                dve.tensor_tensor(num[:, ts, :], msum[:, ts, h * HW:(h + 1) * HW], sums[:, :, HW:VW], ALU.subtract)\
                    .then_inc(direct_num, 1)
                dve.tensor_tensor(num2[:, ts, :], sums[:, :, 0:HW], f[0], ALU.mult).then_inc(read["c"], 1)
                dve.wait_ge(direct_num, o.count(6, n + 1))
                dve.tensor_tensor(num[:, ts, :], num[:, ts, :], f[1], ALU.mult).then_inc(direct_num, 1)
                dve.wait_ge(direct_num, o.count(6, n + 2))
                dve.wait_ge(read["c"], o.count(2 * H, 2 * h + k + 1))
                dve.tensor_tensor(num[:, ts, :], num[:, ts, :], num2[:, ts, :], ALU.add).then_inc(direct_num, 1)

            def outs(kind, h, k):
                return h if h <= DIRECT[kind] and k == 0 else DIRECT[kind] + 2 * (h - DIRECT[kind]) + k

            def head_out(kind, o, h, ts=slice(0, T)):
                cols, tiles = slice(h * DH, (h + 1) * DH), ts.stop - ts.start
                n = outs(kind, h, ts.start // 4)
                if h < DIRECT[kind]:
                    dve.wait_ge(num_made, o.count(4 * (H - 1), 4 * h + 4))
                else:
                    dve.wait_ge(direct_num, o.count(6, 6 * (h - DIRECT[kind]) + 3 * (ts.start // 4) + 3))
                dve.reciprocal(rgat[:, ts], num[:, ts, DH]).then_inc(rgat_made, 1)
                dve.wait_ge(rgat_made, o.count(H + 1, n + 1))
                dve.tensor_tensor(gatout[:, ts, :], num[:, ts, 0:DH], rgat[:, ts].unsqueeze(2).broadcast_to([P, tiles, DH]),
                                  ALU.mult).then_inc(gat_made, 1)
                dve.wait_ge(gat_made, o.count(H + 1, n + 1))
                if h == 0 and (o.turn is not None or o.base > 0):
                    dve.wait_ge(stored, o.count(32))
                ins = dve.tensor_tensor(x3[:, ts, cols], gatout[:, ts, :], x2[:, ts, cols], ALU.add)
                if h == H - 1:
                    ins.then_inc(y_made[2], 1)

            def layer1_out(kind, g, k):
                s = by_tile(slot(kind, "out1", k))
                half = x2[:, 4 * k:4 * k + 4, :]
                dve.wait_ge(full["out1"], g.count(2, k + 1))
                if k == 0:
                    dve.wait_ge(degrees, g.count(3, 3))
                    if kind == "first":
                        dve.wait_ge(late_in, 48)
                for j in range(4):
                    t = 4 * k + j
                    ins = dve.scalar_tensor_tensor(x2[:, t, :], s[:, j, :], rrow[:, t:t + 1], b1_s[:, :], ALU.mult, ALU.add)
                ins.then_inc(read["out1"], 1)
                dve.wait_ge(read["out1"], g.count(2, k + 1))
                dve.scalar_tensor_tensor(half, half, SLOPE1, half, ALU.mult, ALU.max).then_inc(z1_made, 1)
                dve.wait_ge(z1_made, g.count(2, k + 1))
                dve.tensor_tensor(half, half, x1[:, 4 * k:4 * k + 4, :], ALU.add).then_inc(y_made[1], 1)

            def layer3_out(kind, o, k):
                s = by_tile(slot(kind, "out3", k))
                dve.wait_ge(full["out3"], o.count(2, k + 1))
                dve.wait_ge(normed[2], o.count(2, k + 1))
                for j in range(4):
                    t = 4 * k + j
                    ins = dve.scalar_tensor_tensor(x3[:, t, :], s[:, j, :], dcol[o.parity][:, t:t + 1], x3[:, t, :],
                                                   ALU.mult, ALU.add)
                ins.then_inc(y_made[3], 1)

            def split_first_piece(o):
                v = VALS["last"][:, :, 0, :]
                part = [vparts[:, :, 0, n, :] for n in range(3)]
                dve.wait_ge(vals_made, o.count(2 + 2 * NP, 4))
                dve.tensor_copy(part[0], v).then_inc(first_split, 1)
                dve.wait_ge(first_split, 1)
                dve.tensor_tensor(v, v, part[0], ALU.subtract).then_inc(first_split, 1)
                dve.wait_ge(first_split, 2)
                dve.tensor_copy(part[1], v).then_inc(first_split, 1)
                dve.wait_ge(first_split, 3)
                dve.tensor_tensor(part[2], v, part[1], ALU.subtract).then_inc(first_split, 1)

            def layer2_of_last(o):
                kind = "last"
                split_first_piece(o)
                mins(kind, o, 0, range(0, 2))
                take_part(kind, o, 1, 0)
                mins(kind, o, 0, range(2, 5))
                take_part(kind, o, 2, 0)
                take_part(kind, o, 1, 1)
                mins(kind, o, 0, range(5, T))
                take_part(kind, o, 3, 0)
                take_part(kind, o, 2, 1)
                mins(kind, o, 1, range(0, 3))
                take_part(kind, o, 3, 1)
                mins(kind, o, 1, range(3, T))
                sums_of_head(kind, o, 0, 0)
                sums_of_head(kind, o, 0, 1)
                norm_stats(3, o.before(), x3, 0)
                norm_stats(3, o.before(), x3, 1)
                mins(kind, o, 2)
                sums_of_masks(kind, o, 0)
                norm_apply(3, o.before(), x3, 0)
                norm_apply(3, o.before(), x3, 1)
                mins(kind, o, 3, range(0, 4))
                sums_of_masks(kind, o, 1)
                mins(kind, o, 3, range(4, T))

            def last_heads(kind, o):
                head_out(kind, o, 0)
                if kind == "full":
                    sums_of_head(kind, o, 2, 0)
                    sums_of_head(kind, o, 2, 1)
                    head_out(kind, o, 1)
                    head_out(kind, o, 2)
                for h in range(DIRECT[kind], H):
                    for k in range(2):
                        combine_direct(kind, o, h, k)
                        head_out(kind, o, h, slice(4 * k, 4 * k + 4))
                        if h == H - 1:
                            norm_stats(2, o, x3, k)
                split_x3(o, 0)
                split_x3(o, 1)

            def step(kind, g):
                o = g.before()
                if kind == "last":
                    guard_heads(o)
                    layer2_of_last(o)
                    last_heads(kind, o)
                    for k in range(2):
                        layer3_out(kind, o, k)
                        norm_stats(3, o, x3, k)
                    norm_apply(3, o, x3, 0)
                    norm_apply(3, o, x3, 1)
                    return
                dve.wait_ge(read["xT"], g.count(1, 1))
                dve.tensor_copy(xb, xT[:, :]).then_inc(xb_made, 1)
                if kind == "first":
                    make_first_maskb(0)
                dve.wait_ge(read["q"], g.count(1, 1))
                dve.tensor_copy(qb, qT[:, :]).then_inc(qb_made, 1)
                if kind == "first":
                    make_first_maskb(1)
                finish = g.turn is not None or g.base > 1
                guards(kind, g, range(0, 4))
                if kind == "first":
                    guards(kind, g, range(4, T))
                    project_heads()
                else:
                    guard_heads(o)
                    guards(kind, g, range(4, 5))
                    guards(kind, g, range(5, 6))
                    if finish:
                        norm_stats(3, o.before(), x3, 0)
                        norm_stats(3, o.before(), x3, 1)
                    mins(kind, o, 0, range(0, 2))
                    take_part(kind, o, 0, 0)
                    guards(kind, g, range(6, 7))
                    mins(kind, o, 0, range(2, 4))
                    guards(kind, g, range(7, T))
                    take_part(kind, o, 1, 0)
                    take_part(kind, o, 0, 1)
                    mins(kind, o, 0, range(4, 7))
                    take_part(kind, o, 1, 1)
                context(g, 0)
                norm_stats(0, g, x1, 0)
                if kind == "full" and finish:
                    norm_apply(3, o.before(), x3, 0)
                    norm_apply(3, o.before(), x3, 1)
                if kind == "full":
                    mins(kind, o, 0, range(7, T))
                    mins(kind, o, 1)
                norm_apply(0, g, x1, 0)
                split_x1(g, 0)
                context(g, 1)
                norm_stats(0, g, x1, 1)
                if kind == "full":
                    sums_of_masks(kind, o, 0)
                    mins(kind, o, 2)
                    sums_of_masks(kind, o, 1)
                norm_apply(0, g, x1, 1)
                if kind == "full":
                    sums_of_head(kind, o, 0, 0)
                split_x1(g, 1)
                if kind == "full":
                    sums_of_head(kind, o, 0, 1)
                    mins(kind, o, 3, range(0, 4))
                    sums_of_head(kind, o, 1, 0)
                    mins(kind, o, 3, range(4, T))
                    sums_of_head(kind, o, 1, 1)
                    last_heads(kind, o)
                for k in range(2):
                    layer1_out(kind, g, k)
                    norm_stats(1, g, x2, k)
                final = g.turn is None and g.base == NB - 1
                if kind == "full" and not final:
                    layer3_out(kind, o, 0)
                    layer3_out(kind, o, 1)
                norm_apply(1, g, x2, 0)
                norm_apply(1, g, x2, 1)
                if final:
                    layer3_out(kind, o, 0)
                    layer3_out(kind, o, 1)

            program(dve, step)

        @block.tensor
        def _(pe):
            pe.wait_ge(ident_made, 2)

            def query_weights():
                pe.wait_ge(qk_in, 48)
                pe.matmul(Z[:, 0, 0:D], wq_s[:, :], wk_s[:, :], start=True, stop=True)
                pe.matmul(Z[:, 1, 0:1], wk_s[:, :], bqcol[:, 0:1], start=True, stop=True).then_inc(wqk_full, 1)
                pe.wait_ge(act_init, 1)

            def claim(kind, g, name, k):
                n = ORDER[kind].index((name, k))
                if n >= SLOTS:
                    (was, j), of = ORDER[kind][n - SLOTS], g
                elif kind == "first":
                    return slot(kind, name, k)
                elif g.turn is None and g.base == 1:
                    (was, j), of = ORDER["first"][n - SLOTS], g.before()
                else:
                    (was, j), of = ORDER["full"][n - SLOTS], g.before()
                if was in OLDER:
                    of = of.before()
                if was == "out3":
                    pe.wait_ge(y_made[3], of.count(2, j + 1))
                else:
                    pe.wait_ge(read[was], of.count(PER[was], j + 1))
                return slot(kind, name, k)

            def transposes(kind, g, h, name, src):
                s = whole(claim(kind, h, name, 0))
                for t in range(T):
                    last = pe.transpose(s[:, t * P:(t + 1) * P], src[:, t, :], identf[:, :])
                last.then_inc(full[name], 1)

            def project(kind, g, name):
                if name == "xT":
                    pe.wait_ge(x_in, g.count(16, 16))
                    transposes(kind, g, g, "xT", x0)
                elif name == "q":
                    if kind == "first":
                        query_weights()
                    s = claim(kind, g, "q", 0)
                    pe.wait_ge(read["xT"], g.count(1, 1))
                    for c in range(2):
                        last = pe.matmul(s[:, c, :], wqk[:, :], xT[:, c * 512:(c + 1) * 512], start=True, stop=True)
                    last.then_inc(full["q"], 1)
                else:
                    s = by_tile(claim(kind, g, "v", 0))
                    if kind == "first":
                        pe.wait_ge(wv_in, 16)
                    for t in range(T):
                        last = pe.matmul(s[:, t, :], xT[:, t * P:(t + 1) * P], wv_s[:, :], start=True, stop=True)
                    last.then_inc(full["v"], 1)

            def transpose_adj(kind, g, m):
                s = by_tile(claim(kind, g, "at", m))
                if m == 0:
                    if kind == "first":
                        pe.wait_ge(dve_init, 1)
                    for half in adj_in[g.parity]:
                        pe.wait_ge(half, g.count_own(16, 16))
                for t in range(T):
                    last = pe.matmul(s[:, t, :], adjs[g.parity][:, t, m * P:(m + 1) * P], ident16[:, :],
                                     start=True, stop=True)
                last.then_inc(full["at"], 1)

            def guard_scores(kind, g, t):
                s = claim(kind, g, "s", t)
                if t == 0:
                    pe.wait_ge(xb_made, g.count(1, 1))
                    pe.wait_ge(qb_made, g.count(1, 1))
                for c in range(2):
                    last = pe.matmul(s[:, c, :], qb[:, t * P:(t + 1) * P], xb[:, c * 512:(c + 1) * 512],
                                     start=True, stop=True)
                last.then_inc(full["s"], 1)

            def head_inputs(kind, g, name, k):
                o = g.before()
                if name == "x2T":
                    pe.wait_ge(normed[1], o.count(2, 2))
                    transposes(kind, o, g, "x2T", x2)
                elif name == "wh":
                    s = quarters(claim(kind, g, "wh", k))
                    pe.wait_ge(read["x2T"], o.count(1, 1))
                    for j in range(4):
                        t = 4 * k + j
                        last = pe.matmul(s[:, j, 0:D + 2 * H], x2T[:, t * P:(t + 1) * P], wext[:, :], start=True, stop=True)
                    last.then_inc(full["wh"], 1)
                else:
                    if kind == "last":
                        pe.wait_ge(read["agg3"], o.count(2))
                        for c in range(2):
                            last = pe.matmul(Z[:, c, :], wext[:, D + H:D + H + 1].broadcast_to([P, P]),
                                             x2T[:, c * 512:(c + 1) * 512], start=True, stop=True)
                        last.then_inc(sjb_full, 1)
                    s = claim(kind, g, "sj", 0)
                    pe.wait_ge(read["x2T"], o.count(1, 1))
                    for c in range(2):
                        last = pe.matmul(s[0:H, c, :], wext[:, D + H:D + 2 * H], x2T[:, c * 512:(c + 1) * 512],
                                         start=True, stop=True)
                    last.then_inc(full["sj"], 1)

            def scores(kind, g, n):
                c = n // 4
                s = claim(kind, g, "st", n)
                for j in range(2):
                    kt = 2 * (n % 4) + j
                    if kind == "first" and n == 0 and j == 0:
                        pe.wait_ge(dve_init, 1)
                    if n % 4 == 0 and j == 0:
                        pe.wait_ge(guarded, g.count(T, 4 * c + 4))
                    for q in range(4):
                        pe.matmul(s[:, j, q * P:(q + 1) * P], maskb[:, 4 * c + q, kt * P:(kt + 1) * P],
                                  ident16[:, :], start=q == 0, stop=False, skip_group_check=True)
                    last = pe.matmul(s[:, j, :], xT[:, kt * P:(kt + 1) * P], qT[:, c * 512:(c + 1) * 512],
                                     start=False, stop=True, skip_group_check=True)
                last.then_inc(full["st"], 1)

            def context(kind, g, n):
                c = n // 4
                zq = quarters(Z)
                if n == 0:
                    pe.wait_ge(read["v"], g.count(1, 1))
                    if kind == "first":
                        pe.wait_ge(pool_init, 3)
                    if g.turn is not None or g.base > 1:
                        pe.wait_ge(read["agg3"], g.before(2).count(2, 2))
                    if g.turn is not None or g.base > 0:
                        pe.wait_ge(read["agg1"], g.count(1))
                elif n == 4:
                    pe.wait_ge(y_made[0], g.count(2, 1))
                pe.wait_ge(read["st"], g.count(T, n + 1))
                for j in range(2):
                    kt = 2 * (n % 4) + j
                    for q in range(4):
                        last = pe.matmul(zq[:, q, 0:D + 1], probs[:, n % 2, j, q * P:(q + 1) * P], vv[:, kt, :],
                                         start=kt == 0 and q % 2 == 0, stop=kt == T - 1, skip_group_check=True)
                last.then_inc(probs_used, 1)

            def mask_sums(kind, g, k):
                o = g.before()
                s = quarters(claim(kind, g, "mask", k))
                if k == 0:
                    pe.wait_ge(low_made, o.count(NP, len(PIECES[kind]) - SPLIT_BY_DVE[kind]))
                for j in range(4):
                    jt = 4 * k + j
                    for t in range(T):
                        for part in range(3):
                            last = pe.matmul(s[:, j, 0:H * HW], adjs[o.parity][:, t, jt * P:(jt + 1) * P],
                                             vparts[:, t, :, part, HW:VW], start=t == 0 and part == 0,
                                             stop=t == T - 1 and part == 2)
                last.then_inc(full["mask"], 1)

            def head_sums(kind, g, n):
                o = g.before()
                h = n // 2
                c_of = (C_OF if kind == "full" else C_LAST)[h]
                s = quarters(claim(kind, g, "c", n))
                for j in range(4):
                    jt = 4 * (n % 2) + j
                    for t in range(T):
                        if n % 2 == 0 and j == 0:
                            if kind == "last" and t == 0:
                                if h == 0:
                                    pe.wait_ge(first_split, 4)
                                else:
                                    pe.wait_ge(low_made, o.count(NP, h))
                            pe.wait_ge(c_made, o.count(H * T, h * T + t + 1))
                        c_tile = c_of[:, t, jt * P:(jt + 1) * P]
                        if h < DIRECT[kind]:
                            last = pe.matmul(s[:, j, 0:3 * VW], c_tile, vparts[:, t, h, :, :], start=t == 0, stop=t == T - 1)
                        else:
                            for part in range(3):
                                last = pe.matmul(s[:, j, 0:VW], c_tile, vparts[:, t, h, part, :],
                                                 start=t == 0 and part == 0, stop=t == T - 1 and part == 2)
                last.then_inc(full["c"], 1)

            def aggregate(kind, g, of, agg, out, parts, mat, second_half, aggT, weights, inside=None):
                alone = kind == "last" or (kind == "first" and agg == "agg1")
                for n in range(2 * T):
                    c, t = ((n // 4) % 2, n % 4 + 4 * (n // 8)) if alone else (n // T, n % T)
                    if c == 0 and t == 4:
                        pe.wait_ge(*second_half)
                    for part in range(3):
                        last = pe.matmul(Z[:, c, :], parts[:, part, t, :], mat[:, t, c * 512:(c + 1) * 512],
                                         start=t == 0 and part == 0, stop=t == T - 1 and part == 2)
                    if t == T - 1:
                        last.then_inc(full[agg], 1)
                    if c == 0 and t == 1 and inside:
                        inside()
                    if c == 1 and t == (6 if alone else 3):
                        times_weights(kind, g, of, agg, out, aggT, weights, 0)

            def times_weights(kind, g, of, agg, out, aggT, weights, k):
                s = by_tile(claim(kind, g, out, k))
                pe.wait_ge(read[agg], of.count(2, k + 1))
                for j in range(4):
                    t = 4 * k + j
                    last = pe.matmul(s[:, j, :], aggT[:, t * P:(t + 1) * P], weights[:, :], start=True, stop=True)
                last.then_inc(full[out], 1)

            def layer1(kind, g):
                pe.wait_ge(split1, g.count(8, 4))
                pe.wait_ge(y_made[0], g.count(2, 2))
                pe.wait_ge(read["at"], g.count(T, T))
                aggregate(kind, g, g, "agg1", "out1", parts1, adjTs[g.parity], (split1, g.count(8, 8)), agg1T, w1_s)

            def finish_layer1(kind, g):
                times_weights(kind, g, g, "agg1", "out1", agg1T, w1_s, 1)

            def layer3(kind, g):
                o = g.before()
                pe.wait_ge(split3, o.count(10, 5))
                pe.wait_ge(diag_added, o.count(1, 1))
                if kind == "last":
                    pe.wait_ge(sjb_read, 1)
                aggregate(kind, g, o, "agg3", "out3", parts3, adjTs[o.parity], (split3, o.count(10, 10)), agg3T, b3_s,
                          None if kind == "last" else lambda: finish_layer1(kind, g))
                times_weights(kind, g, o, "agg3", "out3", agg3T, b3_s, 1)

            def step(kind, g):
                for name, k in {"first": first_opening, "full": opening, "last": heads_up}[kind]:
                    group(kind, g, name, k)
                if kind != "last":
                    between = between_scores if kind == "full" else first_between
                    for n in range(T):
                        scores(kind, g, n)
                        if between[n]:
                            group(kind, g, *between[n])
                        if n >= 1:
                            context(kind, g, n - 1)
                    context(kind, g, T - 1)
                if kind == "first":
                    pe.wait_ge(late_in, 48)
                else:
                    for name, k in ORDER[kind]:
                        if name == "mask":
                            mask_sums(kind, g, k)
                        elif name == "c":
                            head_sums(kind, g, k)
                if kind != "last":
                    layer1(kind, g)
                if kind == "first":
                    finish_layer1(kind, g)
                    pe.wait_ge(dve_init, 5)
                else:
                    layer3(kind, g)

            def group(kind, g, name, k):
                if name in ("xT", "q", "v"):
                    project(kind, g, name)
                elif name == "at":
                    transpose_adj(kind, g, k)
                elif name == "s":
                    guard_scores(kind, g, k)
                else:
                    head_inputs(kind, g, name, k)

            program(pe, step)


_INS = ['x', 'adj', 'Wq', 'bq', 'Wk', 'WvT', 'bv', 'W1T', 'b1', 'W2', 'a2', 'B3']


def kernel(**inputs):
    import numpy as _np
    import concourse.bacc as _bacc
    from concourse import mybir as _mybir
    from concourse.bass_utils import run_bass_kernel_spmd as _run

    given = {
        'x': inputs['x'], 'adj': inputs['adj'],
        'Wq': inputs['L0_gnn_Wq'], 'bq': inputs['L0_gnn_bq'],
        'Wk': inputs['L0_gnn_Wk'], 'WvT': _np.asarray(inputs['L0_gnn_Wv']).T,
        'bv': inputs['L0_gnn_bv'],
        'W1T': _np.asarray(inputs['L1_gnn_W']).T, 'b1': inputs['L1_gnn_b'],
        'W2': inputs['L2_gnn_W'], 'a2': inputs['L2_gnn_a'], 'B3': inputs['L3_gnn_B'],
    }
    nc = _bacc.Bacc("TRN2", target_bir_lowering=False, num_devices=1)
    arrays, args = {}, []
    for name in _INS:
        a = _np.ascontiguousarray(given[name])
        arrays[f"in_{name}_dram"] = a
        args.append(nc.dram_tensor(f"in_{name}_dram", a.shape, _mybir.dt.from_np(a.dtype), kind="ExternalInput").ap())
    shape = tuple(inputs['x'].shape)
    args.append(nc.dram_tensor("out_0_dram", shape, _mybir.dt.float32, kind="ExternalOutput").ap())
    gnn_kernel(nc, *args)
    r = _run(nc, [arrays], core_ids=[0])
    return r.results[0]["out_0_dram"]
```
